# Optimizing a Trainium2 kernel written in Bass

```python
import numpy as np
import jax
import jax.numpy as jnp

def _softmax(x, axis=-1):
    return jax.nn.softmax(x, axis=axis)

def _gelu(x):
    return jax.nn.gelu(x, approximate=True)

def _silu(x):
    return jax.nn.silu(x)

def _sigmoid(x):
    return jax.nn.sigmoid(x)

def _layernorm(x, axis=-1, eps=1e-05):
    m = jnp.mean(x, axis=axis, keepdims=True)
    v = jnp.var(x, axis=axis, keepdims=True)
    return (x - m) / jnp.sqrt(v + eps)

def _scatter_add(tgt, idx, src, axis=0):
    return tgt.at[idx].add(src)

def _segment_sum(src, seg, n):
    return jax.ops.segment_sum(src, seg, n)
kernel_name = 'mk_macaron_d1_jaxref_r8_84358b'

def setup_inputs(seed: int=0):
    np.random.seed(seed)
    _w = jnp.asarray

    def _L0_attn_setup():
        import jax, jax.numpy as jnp
        import numpy as np
        import math
        B, S, D = (2, 512, 128)
        H, HD = (16, 64)
        WIN = 128
        G = 32
        SCALE = 1.0 / math.sqrt(HD)

        def _forward(x, wq, wk, wv, wo, ws1, bs1, ws2, bs2):
            b, s, d = x.shape
            neg = jnp.finfo(x.dtype).min
            h = jax.nn.gelu(x @ ws1 + bs1, approximate=False)
            scores = (h @ ws2 + bs2).squeeze(-1)
            causal_bs = jnp.triu(jnp.ones((b, s), bool), 1)
            scores = jnp.where(causal_bs, neg, scores)
            _, idx = jax.lax.top_k(scores, min(G, s))
            g_tok = jnp.take_along_axis(x, idx[:, :, None], axis=1)
            q = (x @ wq).reshape(b, s, H, HD).transpose(0, 2, 1, 3)
            k = (x @ wk).reshape(b, s, H, HD).transpose(0, 2, 1, 3)
            v = (x @ wv).reshape(b, s, H, HD).transpose(0, 2, 1, 3)
            gk = (g_tok @ wk).reshape(b, -1, H, HD).transpose(0, 2, 1, 3)
            gv = (g_tok @ wv).reshape(b, -1, H, HD).transpose(0, 2, 1, 3)
            nw = s // WIN
            qw = q.reshape(b, H, nw, WIN, HD)
            kw = k.reshape(b, H, nw, WIN, HD)
            vw = v.reshape(b, H, nw, WIN, HD)
            att = jnp.einsum('bhwqd,bhwkd->bhwqk', qw, kw) * SCALE
            cm = jnp.triu(jnp.ones((WIN, WIN), bool), 1)
            att = jnp.where(cm, neg, att)
            p = jax.nn.softmax(att, axis=-1)
            local_out = jnp.einsum('bhwqk,bhwkd->bhwqd', p, vw).reshape(b, H, s, HD)
            gatt = jnp.einsum('bhsd,bhgd->bhsg', q, gk) * SCALE
            gp = jax.nn.softmax(gatt, axis=-1)
            global_out = jnp.einsum('bhsg,bhgd->bhsd', gp, gv)
            out = (local_out + global_out).transpose(0, 2, 1, 3).reshape(b, s, H * HD)
            return out @ wo
        key = jax.random.key(seed)
        ks = jax.random.split(key, 9)
        w = 0.02
        return {'x': jax.random.normal(ks[0], (B, S, D), jnp.float32), 'wq': jax.random.normal(ks[1], (D, H * HD), jnp.float32) * w, 'wk': jax.random.normal(ks[2], (D, H * HD), jnp.float32) * w, 'wv': jax.random.normal(ks[3], (D, H * HD), jnp.float32) * w, 'wo': jax.random.normal(ks[4], (H * HD, D), jnp.float32) * w, 'ws1': jax.random.normal(ks[5], (D, D // 4), jnp.float32) * w, 'bs1': jnp.zeros((D // 4,), jnp.float32), 'ws2': jax.random.normal(ks[6], (D // 4, 1), jnp.float32) * w, 'bs2': jnp.zeros((1,), jnp.float32)}
    _L0_attn_in = _L0_attn_setup()

    def _L0_ffn_setup():
        import jax, jax.numpy as jnp
        import numpy as np
        B, S, H = (2, 256, 128)
        E, I, K = (8, 512, 2)

        def _moe_forward(x, gate_w, wg, wu, wd):
            b, s, h = x.shape
            x_flat = x.reshape(-1, h)
            logits = x_flat @ gate_w.T
            top_v, top_i = jax.lax.top_k(logits, K)
            probs = jax.nn.softmax(top_v.astype(jnp.float32), axis=-1).astype(logits.dtype)
            one_hot = jax.nn.one_hot(top_i, E, dtype=probs.dtype)
            combine = jnp.einsum('tk,tke->et', probs, one_hot)

            def body(acc, ws):
                wge, wue, wde, we = ws
                hidden = jax.nn.silu(x_flat @ wge.T) * (x_flat @ wue.T)
                return (acc + we[:, None] * (hidden @ wde.T), None)
            out, _ = jax.lax.scan(body, jnp.zeros_like(x_flat), (wg, wu, wd, combine))
            return out.reshape(b, s, h)
        key = jax.random.key(seed)
        ks = jax.random.split(key, 5)
        scale_h = 1.0 / np.sqrt(H)
        scale_i = 1.0 / np.sqrt(I)
        x = jax.random.normal(ks[0], (B, S, H), dtype=jnp.float32)
        gate_w = jax.random.normal(ks[1], (E, H), dtype=jnp.float32) * scale_h
        wg = jax.random.normal(ks[2], (E, I, H), dtype=jnp.float32) * scale_h
        wu = jax.random.normal(ks[3], (E, I, H), dtype=jnp.float32) * scale_h
        wd = jax.random.normal(ks[4], (E, H, I), dtype=jnp.float32) * scale_i
        return {'x': x, 'gate_w': gate_w, 'wg': wg, 'wu': wu, 'wd': wd}
    _L0_ffn_in = _L0_ffn_setup()
    _d = {'L0_attn_x': _L0_attn_in['x'], 'L0_attn_wq': _L0_attn_in['wq'], 'L0_attn_wk': _L0_attn_in['wk'], 'L0_attn_wv': _L0_attn_in['wv'], 'L0_attn_wo': _L0_attn_in['wo'], 'L0_attn_ws1': _L0_attn_in['ws1'], 'L0_attn_bs1': _L0_attn_in['bs1'], 'L0_attn_ws2': _L0_attn_in['ws2'], 'L0_attn_bs2': _L0_attn_in['bs2'], 'L0_ffn_gate_w': _L0_ffn_in['gate_w'], 'L0_ffn_wg': _L0_ffn_in['wg'], 'L0_ffn_wu': _L0_ffn_in['wu'], 'L0_ffn_wd': _L0_ffn_in['wd']}
    _x0 = _d['L0_attn_x']
    _d['L0_attn_x'] = jax.random.normal(jax.random.fold_in(jax.random.key(seed), 1), (8, 512, 128), dtype=_x0.dtype)
    del _x0
    return _d

def reference(L0_attn_x, L0_attn_wq, L0_attn_wk, L0_attn_wv, L0_attn_wo, L0_attn_ws1, L0_attn_bs1, L0_attn_ws2, L0_attn_bs2, L0_ffn_gate_w, L0_ffn_wg, L0_ffn_wu, L0_ffn_wd):

    def _L0_attn_ref(x, wq, wk, wv, wo, ws1, bs1, ws2, bs2):
        import jax, jax.numpy as jnp
        import numpy as np
        import math
        B, S, D = (2, 512, 128)
        H, HD = (16, 64)
        WIN = 128
        G = 32
        SCALE = 1.0 / math.sqrt(HD)

        def _forward(x, wq, wk, wv, wo, ws1, bs1, ws2, bs2):
            b, s, d = x.shape
            neg = jnp.finfo(x.dtype).min
            h = jax.nn.gelu(x @ ws1 + bs1, approximate=False)
            scores = (h @ ws2 + bs2).squeeze(-1)
            causal_bs = jnp.triu(jnp.ones((b, s), bool), 1)
            scores = jnp.where(causal_bs, neg, scores)
            _, idx = jax.lax.top_k(scores, min(G, s))
            g_tok = jnp.take_along_axis(x, idx[:, :, None], axis=1)
            q = (x @ wq).reshape(b, s, H, HD).transpose(0, 2, 1, 3)
            k = (x @ wk).reshape(b, s, H, HD).transpose(0, 2, 1, 3)
            v = (x @ wv).reshape(b, s, H, HD).transpose(0, 2, 1, 3)
            gk = (g_tok @ wk).reshape(b, -1, H, HD).transpose(0, 2, 1, 3)
            gv = (g_tok @ wv).reshape(b, -1, H, HD).transpose(0, 2, 1, 3)
            nw = s // WIN
            qw = q.reshape(b, H, nw, WIN, HD)
            kw = k.reshape(b, H, nw, WIN, HD)
            vw = v.reshape(b, H, nw, WIN, HD)
            att = jnp.einsum('bhwqd,bhwkd->bhwqk', qw, kw) * SCALE
            cm = jnp.triu(jnp.ones((WIN, WIN), bool), 1)
            att = jnp.where(cm, neg, att)
            p = jax.nn.softmax(att, axis=-1)
            local_out = jnp.einsum('bhwqk,bhwkd->bhwqd', p, vw).reshape(b, H, s, HD)
            gatt = jnp.einsum('bhsd,bhgd->bhsg', q, gk) * SCALE
            gp = jax.nn.softmax(gatt, axis=-1)
            global_out = jnp.einsum('bhsg,bhgd->bhsd', gp, gv)
            out = (local_out + global_out).transpose(0, 2, 1, 3).reshape(b, s, H * HD)
            return out @ wo
        return _forward(x, wq, wk, wv, wo, ws1, bs1, ws2, bs2)

    def _L0_ffn_ref(x, gate_w, wg, wu, wd):
        import jax, jax.numpy as jnp
        import numpy as np
        B, S, H = (2, 256, 128)
        E, I, K = (8, 512, 2)

        def _moe_forward(x, gate_w, wg, wu, wd):
            b, s, h = x.shape
            x_flat = x.reshape(-1, h)
            logits = x_flat @ gate_w.T
            top_v, top_i = jax.lax.top_k(logits, K)
            probs = jax.nn.softmax(top_v.astype(jnp.float32), axis=-1).astype(logits.dtype)
            one_hot = jax.nn.one_hot(top_i, E, dtype=probs.dtype)
            combine = jnp.einsum('tk,tke->et', probs, one_hot)

            def body(acc, ws):
                wge, wue, wde, we = ws
                hidden = jax.nn.silu(x_flat @ wge.T) * (x_flat @ wue.T)
                return (acc + we[:, None] * (hidden @ wde.T), None)
            out, _ = jax.lax.scan(body, jnp.zeros_like(x_flat), (wg, wu, wd, combine))
            return out.reshape(b, s, h)
        return _moe_forward(x, gate_w, wg, wu, wd)
    x = L0_attn_x
    x = x + 0.5 * _L0_ffn_ref(_layernorm(x, axis=-1), L0_ffn_gate_w, L0_ffn_wg, L0_ffn_wu, L0_ffn_wd)
    x = x + _L0_attn_ref(_layernorm(x, axis=-1), L0_attn_wq, L0_attn_wk, L0_attn_wv, L0_attn_wo, L0_attn_ws1, L0_attn_bs1, L0_attn_ws2, L0_attn_bs2)
    x = x + 0.5 * _L0_ffn_ref(_layernorm(x, axis=-1), L0_ffn_gate_w, L0_ffn_wg, L0_ffn_wu, L0_ffn_wd)
    return x

_drawn_inputs = setup_inputs


def setup_inputs(seed=0):
    import zlib

    import numpy as np

    out = dict(_drawn_inputs(seed))
    spreads = {'L0_attn_bs1': (0.0, 0.8)}
    factors = {'L0_attn_wq': 6.807, 'L0_attn_wk': 7.294, 'L0_attn_ws1': 8.0, 'L0_attn_ws2': 8.0}
    for name, (base, spread) in spreads.items():
        noise = np.random.default_rng([zlib.crc32(name.encode()), seed]).standard_normal(out[name].shape)
        drawn = base * np.exp(spread * noise) if base else spread * noise
        out[name] = jnp.asarray(drawn.astype(out[name].dtype))
    for name, factor in factors.items():
        out[name] = (out[name] * factor).astype(out[name].dtype)
    return out
```

```python
import numpy as np
import concourse.bass as bass
from concourse import mybir
from concourse.alu_op_type import AluOpType as ALU
from contextlib import ExitStack

F32 = mybir.dt.float32
F32R = mybir.dt.float32r
U32 = mybir.dt.uint32
ACT = mybir.ActivationFunctionType
AX = mybir.AxisListType

B, S, D = 8, 512, 128
T = B * S
P = 128
NT = T // P
CH = T // S
TPC = S // P
E, I = 8, 512
J = I // P
H, HD = 16, 64
HP = H * HD // P
WIN = 128
NW = S // WIN
G = 32
SH = D // 4
CAND = B + G
SC = 2 * WIN + 2 * G
EPS = 1e-5
SCALE = 1.0 / HD ** 0.5
TAKEN = float(np.finfo(np.float32).min)
MASKED = float(np.nextafter(np.float32(TAKEN), np.float32(0)))


def hold(eng, buf):
    eng.sem_inc(buf["held"], 1)


START = 1


def start(sp, sems):
    for sem in sems:
        sp.sem_inc(sem, START)


class Scope:

    def __init__(self, nc, sems):
        self.nc, self.sems, self.stack = nc, sems, ExitStack()

    def sb(self, name, shape, dt=F32):
        return self.stack.enter_context(self.nc.sbuf_tensor(name, shape, dt))

    def ps(self, name, shape, dt=F32):
        return self.stack.enter_context(self.nc.psum_tensor(name, shape, dt))

    def sem(self, name):
        return self.sems.enter_context(self.nc.semaphore(name))


def load_constants(nc, sems, buf, dram):
    loaded = sems.enter_context(nc.semaphore("start_loaded"))
    buf["held"] = sems.enter_context(nc.semaphore("held"))
    with nc.Block() as block:
        @block.sync
        def _(sp):
            sp.dma_start(buf["X"][:], dram["x"].rearrange("(t p) d -> p t d", p=P)).then_inc(loaded, 16)
            sp.dma_start(buf["ident"][:], dram["ident"]).then_inc(loaded, 16)
            sp.dma_start(buf["gate"][:], dram["gate"]).then_inc(loaded, 16)
            sp.dma_start(buf["iota8"][:], dram["iota8"]).then_inc(loaded, 16)
            sp.wait_ge(loaded, 64)


def norm_stage(nc, sems, buf, dram, tag, coef, route, heads, out=None):
    sc = Scope(nc, sems)
    X, acc, ident = buf["X"], buf["acc"], buf["ident"]
    xn_hi, xn_lo, logits = buf["xn_hi"], buf["xn_lo"], buf["logits"]
    norm = out is None
    with sc.stack:
        acc_chunk = sc.sb(f"acc_chunk{tag}", [P, S])
        x_norm = sc.sb(f"x_norm{tag}", [P, TPC, D])
        xnt = sc.sb(f"xnt{tag}", [P, S])
        stats = sc.sb(f"stats{tag}", [P, TPC, 6])
        mean_var = sc.sb(f"mean_var{tag}", [P, TPC, 2])
        std = sc.sb(f"std{tag}", [P, TPC])
        rstd = sc.sb(f"rstd{tag}", [P, TPC])
        eps = sc.sb(f"eps{tag}", [P, 1])
        acc_tok = sc.ps(f"acc_tok{tag}", [P, TPC, D])
        xnt_ps = sc.ps(f"xnt_ps{tag}", [P, S])
        lg_ps = sc.ps(f"lg_ps{tag}", [P, TPC, E])
        names = ["acc_staged", "acc_turned", "x_updated", "stats_done", "aggr_done", "std_done", "rstd_done",
                 "normed", "turned", "hi_done", "lo_done", "xnt_done", "logits_done", "logits_kept", "stored", "eps_set"]
        s = {n: sc.sem(f"{n}{tag}") for n in names}
        with nc.Block() as block:
            @block.gpsimd
            def _(pool):
                if coef:
                    with pool.Fori(0, CH) as c:
                        pool.wait_ge(s["acc_turned"], START + c)
                        hold(pool, buf)
                        nc.gpsimd.tensor_copy(acc_chunk[:], acc[:, bass.ts(c, S)]).then_inc(s["acc_staged"], 1)

            @block.tensor
            def _(pe):
                with pe.Fori(0, CH) as c:
                    if coef:
                        pe.wait_ge(s["acc_staged"], START + c + 1)
                        pe.wait_ge(s["x_updated"], START + c)
                        for t in range(TPC):
                            last = nc.tensor.transpose(acc_tok[:, t, :], acc_chunk[:, t * P:(t + 1) * P], ident[:])
                        last.then_inc(s["acc_turned"], 1)
                    if norm:
                        pe.wait_ge(s["normed"], START + TPC * c + TPC)
                        pe.wait_ge(s["lo_done"], START + c)
                        if route:
                            pe.wait_ge(s["xnt_done"], START + c)
                        for t in range(TPC):
                            last = nc.tensor.transpose(xnt_ps[:, t * P:(t + 1) * P], x_norm[:, t, :], ident[:])
                        last.then_inc(s["turned"], 1)
                    if route:
                        pe.wait_ge(s["xnt_done"], START + c + 1)
                        pe.wait_ge(s["logits_kept"], START + c)
                        for t in range(TPC):
                            last = nc.tensor.matmul(lg_ps[:, t, :], xnt[:, t * P:(t + 1) * P], buf["gate"][:],
                                                    start=True, stop=True)
                        last.then_inc(s["logits_done"], 1)

            @block.scalar
            def _(act):
                if not norm:
                    return
                act.wait_ge(s["eps_set"], START + 1)
                with act.Fori(0, CH) as c:
                    act.wait_ge(s["aggr_done"], START + TPC * c + TPC)
                    act.wait_ge(s["rstd_done"], START + c)
                    nc.scalar.activation(std[:], mean_var[:, :, 1], ACT.Sqrt, bias=eps[:]).then_inc(s["std_done"], 1)
                    act.wait_ge(s["turned"], START + c + 1)
                    nc.scalar.copy(xn_hi[:, bass.ts(c, S)], xnt_ps[:]).then_inc(s["hi_done"], 1)
                    if route:
                        act.wait_ge(s["logits_done"], START + c)
                        nc.scalar.copy(xnt[:], xnt_ps[:]).then_inc(s["xnt_done"], 1)

            @block.vector
            def _(dve):
                if norm:
                    nc.vector.memset(eps[:], EPS).then_inc(s["eps_set"], 1)
                with dve.Fori(0, CH) as c:
                    x_c = X[:, bass.ts(c, TPC), :]
                    if coef:
                        dve.wait_ge(s["acc_turned"], START + c + 1)
                        nc.vector.scalar_tensor_tensor(x_c, acc_tok[:], coef, x_c, ALU.mult, ALU.add)\
                            .then_inc(s["x_updated"], 1)
                        dve.wait_ge(s["x_updated"], START + c + 1)
                    if norm:
                        dve.wait_ge(s["std_done"], START + c)
                        hold(dve, buf)
                        for t in range(TPC):
                            nc.vector.bn_stats(stats[:, t, :], X[:, TPC * c + t, :]).then_inc(s["stats_done"], 1)
                        dve.wait_ge(s["stats_done"], START + TPC * c + TPC)
                        hold(dve, buf)
                        for t in range(TPC):
                            nc.vector.bn_aggr(mean_var[:, t, :], stats[:, t, :]).then_inc(s["aggr_done"], 1)
                        dve.wait_ge(s["std_done"], START + c + 1)
                        nc.vector.reciprocal(rstd[:], std[:]).then_inc(s["rstd_done"], 1)
                        dve.wait_ge(s["rstd_done"], START + c + 1)
                        dve.wait_ge(s["turned"], START + c)
                        for t in range(TPC):
                            nc.vector.tensor_scalar(x_norm[:, t, :], X[:, TPC * c + t, :], mean_var[:, t, 0:1],
                                                    rstd[:, t:t + 1], ALU.subtract, ALU.mult).then_inc(s["normed"], 1)
                        if heads:
                            dve.wait_ge(s["normed"], START + TPC * c + 1)
                            nc.vector.tensor_copy(buf["xn_head"][:, c, :], x_norm[0:CAND, 0, :])
                        dve.wait_ge(s["xnt_done" if route else "hi_done"], START + c + 1)
                        nc.vector.tensor_tensor(xn_lo[:, bass.ts(c, S)], xnt_ps[:],
                                                xn_hi[:, bass.ts(c, S)].bitcast(F32), ALU.subtract)\
                            .then_inc(s["lo_done"], 1)
                    if route:
                        dve.wait_ge(s["logits_done"], START + c + 1)
                        nc.vector.tensor_copy(logits[:, bass.ts(c, TPC), :], lg_ps[:]).then_inc(s["logits_kept"], 1)

            @block.sync
            def _(sp):
                start(sp, [s[n] for n in names if n != "stored"])
                if not norm:
                    out_v = out.rearrange("(c t p) d -> c p t d", p=P, t=TPC)
                    with sp.Fori(0, CH) as c:
                        sp.wait_ge(s["x_updated"], START + c + 1)
                        sp.dma_start(out_v[c], X[:, bass.ts(c, TPC), :]).then_inc(s["stored"], 16)
                    sp.wait_ge(s["stored"], 16 * CH)


def route_stage(nc, sems, buf, dram, tag):
    sc = Scope(nc, sems)
    logits, ident = buf["logits"], buf["ident"]
    with sc.stack:
        top = sc.sb(f"top{tag}", [P, NT, 8])
        top_i = sc.sb(f"top_i{tag}", [P, NT, 8], U32)
        pick = sc.sb(f"pick{tag}", [P, NT, 2])
        diff = sc.sb(f"diff{tag}", [P, NT])
        e2 = sc.sb(f"e2{tag}", [P, NT])
        den = sc.sb(f"den{tag}", [P, NT])
        w = sc.sb(f"w{tag}", [P, NT, 2])
        oh = sc.sb(f"oh{tag}", [P, NT, 2, E])
        comb = sc.sb(f"comb{tag}", [P, NT, E])
        comb_t = sc.sb(f"comb_t{tag}", [E, T])
        turn_ps = [sc.ps(f"turn_ps{k}{tag}", [E, S]) for k in range(2)]
        chain, e2_done, comb_done, turned, kept, stored = (
            sc.sem(f"{n}{tag}") for n in ("r_chain", "r_e2_done", "r_comb_done", "r_turned", "r_kept", "r_stored"))
        with nc.Block() as block:
            @block.vector
            def _(dve):
                n = [0]

                def step(ins):
                    n[0] += 1
                    ins.then_inc(chain, 1)

                def settled():
                    dve.wait_ge(chain, n[0])

                for t in range(NT):
                    step(nc.vector.max(top[:, t, :], logits[:, t, :]))
                settled()
                for t in range(NT):
                    step(nc.vector.max_index(top_i[:, t, :], top[:, t, :], logits[:, t, :]))
                step(nc.vector.tensor_tensor(diff[:], top[:, :, 1], top[:, :, 0], ALU.subtract))
                settled()
                step(nc.vector.tensor_copy(pick[:], top_i[:, :, 0:2]))
                dve.wait_ge(e2_done, 1)
                step(nc.vector.tensor_scalar_add(den[:], e2[:], 1.0))
                settled()
                step(nc.vector.reciprocal(w[:, :, 0], den[:]))
                for k in range(2):
                    step(nc.vector.tensor_tensor(oh[:, :, k, :], buf["iota8"][:],
                                                 pick[:, :, k:k + 1].broadcast_to([P, NT, E]), ALU.is_equal))
                settled()
                step(nc.vector.tensor_tensor(w[:, :, 1], e2[:], w[:, :, 0], ALU.mult))
                settled()
                for k in range(2):
                    step(nc.vector.tensor_tensor(oh[:, :, k, :], oh[:, :, k, :],
                                                 w[:, :, k:k + 1].broadcast_to([P, NT, E]), ALU.mult))
                settled()
                nc.vector.tensor_tensor(comb[:], oh[:, :, 0, :], oh[:, :, 1, :], ALU.add).then_inc(comb_done, 1)
                for c in range(CH):
                    dve.wait_ge(turned, c + 1)
                    nc.vector.tensor_copy(comb_t[:, c * S:(c + 1) * S], turn_ps[c % 2][:]).then_inc(kept, 1)

            @block.scalar
            def _(act):
                act.wait_ge(chain, 2 * NT + 1)
                nc.scalar.activation(e2[:], diff[:], ACT.Exp).then_inc(e2_done, 1)

            @block.tensor
            def _(pe):
                pe.wait_ge(comb_done, 1)
                for c in range(CH):
                    if c >= 2:
                        pe.wait_ge(kept, c - 1)
                    for t in range(TPC):
                        last = nc.tensor.transpose(turn_ps[c % 2][:, t * P:(t + 1) * P], comb[:, c * TPC + t, :],
                                                   ident[:])
                    last.then_inc(turned, 1)

            @block.sync
            def _(sp):
                sp.wait_ge(kept, CH)
                sp.dma_start(dram["comb"][:, :], comb_t[:]).then_inc(stored, 16)
                sp.wait_ge(stored, 16)


def ffn_stage(nc, sems, buf, dram, tag):
    sc = Scope(nc, sems)
    acc, xn_hi, xn_lo = buf["acc"], buf["xn_hi"], buf["xn_lo"]
    WC = 3 * I
    with sc.stack:
        stage = [sc.sb(f"w_stage{k}{tag}", [P, WC]) for k in range(2)]
        w_hi = [sc.sb(f"w_hi{k}{tag}", [P, WC], F32R) for k in range(2)]
        w_lo = [sc.sb(f"w_lo{k}{tag}", [P, WC], F32R) for k in range(2)]
        spread = [sc.sb(f"spread{k}{tag}", [P, T]) for k in range(2)]
        silu = sc.sb(f"silu{tag}", [P, 2, S])
        hid = sc.sb(f"hid{tag}", [P, 2, S])
        hid_hi = sc.sb(f"hid_hi{tag}", [P, J, S], F32R)
        hid_lo = sc.sb(f"hid_lo{tag}", [P, J, S], F32R)
        scaled = sc.sb(f"scaled{tag}", [P, S])
        gate_ps = [sc.ps(f"gate_ps{k}{tag}", [P, S]) for k in range(2)]
        up_ps = [sc.ps(f"up_ps{k}{tag}", [P, S]) for k in range(2)]
        y_ps = sc.ps(f"y_ps{tag}", [P, S])
        w_in = [sc.sem(f"w_in{k}{tag}") for k in range(2)]
        spread_in = [sc.sem(f"spread_in{k}{tag}") for k in range(2)]
        names = ["w_hi_done", "w_lo_done", "gate_ready", "up_ready", "silu_done", "hid_done", "hid_hi_done",
                 "hid_lo_done", "y_ready", "scaled_done", "acc_done"]
        s = {n: sc.sem(f"f_{n}{tag}") for n in names}
        with nc.Block() as block:
            @block.sync
            def _(sp):
                for e in range(2):
                    sp.dma_start(stage[e][:], dram["w_ffn"][e]).then_inc(w_in[e], 16)
                    sp.dma_start(spread[e][:], dram["comb"][e, :].partition_broadcast(P)).then_inc(spread_in[e], 16)
                start(sp, s.values())
                with sp.Fori(0, E // 2 - 1) as pair:
                    for k in range(2):
                        e = 2 * pair + k
                        sp.wait_ge(s["w_lo_done"], START + e + 1)
                        sp.dma_start(stage[k][:], dram["w_ffn"][e + 2]).then_inc(w_in[k], 16)
                        sp.wait_ge(s["scaled_done"], START + CH * (e + 1))
                        sp.dma_start(spread[k][:], dram["comb"][e + 2, :].partition_broadcast(P))\
                            .then_inc(spread_in[k], 16)

            @block.gpsimd
            def _(pool):
                def split(e, k, visit):
                    pool.wait_ge(w_in[k], 16 * (visit + 1))
                    hold(pool, buf)
                    nc.gpsimd.tensor_copy(w_hi[k][:], stage[k][:]).then_inc(s["w_hi_done"], 1)
                    pool.wait_ge(s["w_hi_done"], START + e + 1)
                    nc.gpsimd.tensor_tensor(w_lo[k][:], stage[k][:], w_hi[k][:].bitcast(F32), ALU.subtract)\
                        .then_inc(s["w_lo_done"], 1)

                def add_up(e):
                    with pool.Fori(0, CH) as c:
                        pool.wait_ge(s["scaled_done"], START + CH * e + c + 1)
                        nc.gpsimd.tensor_tensor(acc[:, bass.ts(c, S)], acc[:, bass.ts(c, S)], scaled[:], ALU.add)\
                            .then_inc(s["acc_done"], 1)

                nc.gpsimd.memset(acc[:], 0.0).then_inc(s["acc_done"], 1)
                split(0, 0, 0)
                pool.wait_ge(s["acc_done"], START + 1)
                with pool.Fori(0, E // 2 - 1) as pair:
                    pool.wait_ge(s["y_ready"], START + CH * 2 * pair)
                    split(2 * pair + 1, 1, pair)
                    add_up(2 * pair)
                    pool.wait_ge(s["y_ready"], START + CH * (2 * pair + 1))
                    split(2 * pair + 2, 0, pair + 1)
                    add_up(2 * pair + 1)
                pool.wait_ge(s["y_ready"], START + CH * (E - 2))
                split(E - 1, 1, E // 2 - 1)
                add_up(E - 2)
                add_up(E - 1)

            @block.tensor
            def _(pe):
                with pe.Fori(0, E // 2) as pair:
                    for k in range(2):
                        pe.wait_ge(s["w_lo_done"], START + 2 * pair + k + 1)
                        hold(pe, buf)

                        def three(out, col, hi, lo, first=True, last=True):
                            w_h, w_l = w_hi[k][:, col:col + P], w_lo[k][:, col:col + P]
                            nc.tensor.matmul(out, w_h, hi, start=first, stop=False)
                            nc.tensor.matmul(out, w_h, lo, start=False, stop=False)
                            return nc.tensor.matmul(out, w_l, hi, start=False, stop=last)

                        with pe.Fori(0, CH) as c:
                            n = (2 * pair + k) * CH + c
                            hi, lo = xn_hi[:, bass.ts(c, S)], xn_lo[:, bass.ts(c, S)]
                            for j in range(J):
                                pe.wait_ge(s["hid_done"], START + J * n + max(j - 1, 0))
                                three(gate_ps[j % 2][:], j * P, hi, lo).then_inc(s["gate_ready"], 1)
                                three(up_ps[j % 2][:], I + j * P, hi, lo).then_inc(s["up_ready"], 1)
                            pe.wait_ge(s["scaled_done"], START + n)
                            for j in range(J):
                                pe.wait_ge(s["hid_lo_done"], START + J * n + j + 1)
                                last = three(y_ps[:], 2 * I + j * P, hid_hi[:, j, :], hid_lo[:, j, :],
                                             j == 0, j == J - 1)
                            last.then_inc(s["y_ready"], 1)

            @block.scalar
            def _(act):
                with act.Fori(0, E * CH) as n:
                    def gate(j):
                        act.wait_ge(s["gate_ready"], START + J * n + j + 1)
                        act.wait_ge(s["hid_done"], START + J * n + max(j - 1, 0))
                        nc.scalar.activation(silu[:, j % 2, :], gate_ps[j % 2][:], ACT.Silu).then_inc(s["silu_done"], 1)

                    def round_hidden(j):
                        act.wait_ge(s["hid_done"], START + J * n + j + 1)
                        act.wait_ge(s["y_ready"], START + n)
                        nc.scalar.copy(hid_hi[:, j, :], hid[:, j % 2, :]).then_inc(s["hid_hi_done"], 1)

                    gate(0)
                    for j in range(1, J):
                        gate(j)
                        round_hidden(j - 1)
                    round_hidden(J - 1)

            @block.vector
            def _(dve):
                with dve.Fori(0, E // 2) as pair:
                    for k in range(2):
                        dve.wait_ge(spread_in[k], 16 * (pair + 1))
                        hold(dve, buf)
                        with dve.Fori(0, CH) as c:
                            n = (2 * pair + k) * CH + c

                            def multiply(j):
                                dve.wait_ge(s["silu_done"], START + J * n + j + 1)
                                dve.wait_ge(s["up_ready"], START + J * n + j + 1)
                                dve.wait_ge(s["hid_lo_done"], START + J * n + max(j - 1, 0))
                                nc.vector.tensor_tensor(hid[:, j % 2, :], up_ps[j % 2][:], silu[:, j % 2, :], ALU.mult)\
                                    .then_inc(s["hid_done"], 1)

                            def rest(j):
                                dve.wait_ge(s["hid_hi_done"], START + J * n + j + 1)
                                nc.vector.tensor_tensor(hid_lo[:, j, :], hid[:, j % 2, :],
                                                        hid_hi[:, j, :].bitcast(F32), ALU.subtract)\
                                    .then_inc(s["hid_lo_done"], 1)

                            multiply(0)
                            for j in range(1, J):
                                multiply(j)
                                rest(j - 1)
                            rest(J - 1)
                            dve.wait_ge(s["y_ready"], START + n + 1)
                            dve.wait_ge(s["acc_done"], START + n + 1)
                            nc.vector.tensor_tensor(scaled[:], y_ps[:], spread[k][:, bass.ts(c, S)], ALU.mult)\
                                .then_inc(s["scaled_done"], 1)


def select_stage(nc, sems, buf, dram):
    sc = Scope(nc, sems)
    with sc.stack:
        ws1 = sc.sb("ws1", [D, SH])
        bs1 = sc.sb("bs1", [SH, 1])
        ws2 = sc.sb("ws2", [SH, 1])
        bs2 = sc.sb("bs2", [B, 1])
        iota_p = sc.sb("iota_p", [CAND, 1])
        block_b = sc.sb("block_b", [B, B, G])
        xs = sc.sb("xs", [D, B, B])
        hid = sc.sb("sel_hid", [SH, B, B])
        raw = sc.sb("raw", [B, B])
        score = sc.sb("score", [B, 4, CAND])
        best = sc.sb("best", [B, G])
        best_i = sc.sb("best_i", [B, G], U32)
        best_f = sc.sb("best_f", [B, G])
        wide = sc.sb("wide", [B, B, G])
        ones = sc.sb("ones", [B, CAND])
        onehot = sc.sb("onehot", [CAND, B, G])
        hid_ps = sc.ps("sel_hid_ps", [SH, B * B])
        score_ps = sc.ps("score_ps", [B, B])
        idx_ps = sc.ps("idx_ps", [CAND, B * G])
        xg_ps = sc.ps("xg_ps", [D, B, G])
        xg = buf["xg"]
        v_chain, loaded, xs_done, hid_ready, gelu_done, score_ready, masked, wide_done, idx_ready, onehot_done, \
            xg_ready, xg_hi_done, xg_done = (sc.sem(f"sel_{n}") for n in (
                "v_chain", "loaded", "xs_done", "hid_ready", "gelu_done", "score_ready", "masked", "wide_done",
                "idx_ready", "onehot_done", "xg_ready", "xg_hi_done", "xg_done"))
        raw_done = sc.sem("sel_raw_done")
        with nc.Block() as block:
            @block.sync
            def _(sp):
                sp.dma_start(ws1[:], dram["ws1"]).then_inc(loaded, 16)
                sp.dma_start(bs1[:], dram["bs1"].unsqueeze(1)).then_inc(loaded, 16)
                sp.dma_start(ws2[:], dram["ws2"]).then_inc(loaded, 16)
                sp.dma_start(bs2[:], dram["bs2"].partition_broadcast(B)).then_inc(loaded, 16)
                sp.dma_start(iota_p[:], dram["iota_p"]).then_inc(loaded, 16)
                sp.dma_start(block_b[:], dram["block_b"]).then_inc(loaded, 16)

            @block.gpsimd
            def _(pool):
                pool.wait_ge(raw_done, 1)
                nc.gpsimd.affine_select(out=score[:, 0, 0:B], in_=raw[:], pattern=[[-1, B]], compare_op=ALU.is_ge,
                                        fill=MASKED, base=0, channel_multiplier=1).then_inc(masked, 1)

            @block.tensor
            def _(pe):
                pe.wait_ge(loaded, 96)
                pe.wait_ge(xs_done, 1)
                nc.tensor.matmul(hid_ps[:], ws1[:], xs[:], start=True, stop=True).then_inc(hid_ready, 1)
                pe.wait_ge(gelu_done, 1)
                for j in range(B):
                    last = nc.tensor.matmul(score_ps[:, j:j + 1], hid[:, :, j], ws2[:], start=True, stop=True)
                last.then_inc(score_ready, 1)
                pe.wait_ge(wide_done, 1)
                nc.tensor.matmul(idx_ps[:], ones[:], wide[:], start=True, stop=True).then_inc(idx_ready, 1)
                pe.wait_ge(onehot_done, 1)
                for b in range(B):
                    last = nc.tensor.matmul(xg_ps[:, b, :], buf["xn_head"][:, b, :], onehot[:, b, :],
                                            start=True, stop=True)
                last.then_inc(xg_ready, 1)

            @block.scalar
            def _(act):
                act.wait_ge(hid_ready, 1)
                act.wait_ge(loaded, 96)
                nc.scalar.activation(hid[:], hid_ps[:].rearrange("p (b j) -> p b j", b=B), ACT.Gelu, bias=bs1[:])\
                    .then_inc(gelu_done, 1)
                act.wait_ge(xg_ready, 1)
                nc.scalar.copy(xg[:, :, 0, 0:G], xg_ps[:]).then_inc(xg_hi_done, 1)

            @block.vector
            def _(dve):
                n = [0]

                def step(ins):
                    n[0] += 1
                    ins.then_inc(v_chain, 1)
                    dve.wait_ge(v_chain, n[0])

                hi = buf["xn_hi"][:].rearrange("p (b s) -> p b s", b=B)[:, :, 0:B].bitcast(F32)
                lo = buf["xn_lo"][:].rearrange("p (b s) -> p b s", b=B)[:, :, 0:B].bitcast(F32)
                nc.vector.tensor_tensor(xs[:], hi, lo, ALU.add).then_inc(xs_done, 1)
                step(nc.vector.memset(score[:, 0, B:CAND], MASKED))
                step(nc.vector.memset(ones[:], 1.0))
                dve.wait_ge(score_ready, 1)
                dve.wait_ge(loaded, 96)
                nc.vector.tensor_scalar(raw[:], score_ps[:], bs2[:], MASKED, ALU.add, ALU.max).then_inc(raw_done, 1)
                dve.wait_ge(masked, 1)
                for r in range(G // 8):
                    m = best[:, 8 * r:8 * r + 8]
                    step(nc.vector.max(m, score[:, r, :]))
                    step(nc.vector.max_index(best_i[:, 8 * r:8 * r + 8], m, score[:, r, :]))
                    if r < G // 8 - 1:
                        step(nc.vector.match_replace(score[:, r + 1, :], m, score[:, r, :], TAKEN))
                step(nc.vector.tensor_copy(best_f[:], best_i[:]))
                nc.vector.tensor_tensor(wide[:], block_b[:], best_f[:].unsqueeze(1).broadcast_to([B, B, G]), ALU.mult)\
                    .then_inc(wide_done, 1)
                dve.wait_ge(idx_ready, 1)
                nc.vector.tensor_scalar(onehot[:], idx_ps[:].rearrange("p (b g) -> p b g", b=B), iota_p[:], None,
                                        ALU.is_equal).then_inc(onehot_done, 1)
                dve.wait_ge(xg_hi_done, 1)
                step(nc.vector.tensor_tensor(xg[:, :, 1, 0:G], xg_ps[:], xg[:, :, 0, 0:G].bitcast(F32), ALU.subtract))
                step(nc.vector.tensor_copy(xg[:, :, :, G:2 * G].bitcast(F32), xg[:, :, :, 0:G].bitcast(F32)))
                step(nc.vector.tensor_copy(xg[:, :, :, 2 * G:4 * G].bitcast(F32), xg[:, :, :, 0:2 * G].bitcast(F32)))


def attention_stage(nc, sems, buf, dram):
    sc = Scope(nc, sems)
    acc, ident = buf["acc"], buf["ident"]
    U = B * HP
    Q, K, V = range(3)
    with sc.stack:
        w_all = sc.sb("w_all", [P, HP, 6, P], F32R)
        w_raw = sc.sb("w_raw", [P, 2, 3, P])
        w_st = [sc.sb(f"w_st{k}", [P, 6, P], F32R) for k in range(2)]
        wo_st = [sc.sb(f"wo_st{k}", [P, P]) for k in range(2)]
        xst = sc.sb("xst", [P, 2, S], F32R)
        xgst = sc.sb("xgst", [P, 2, P], F32R)
        q_t = [sc.sb(f"q_t{k}", [P, S]) for k in range(2)]
        k_blk = [sc.sb(f"k_blk{k}", [P, NW, SC]) for k in range(2)]
        v_sb = [sc.sb(f"v_sb{k}", [P, NW, P]) for k in range(2)]
        gv_blk = [sc.sb(f"gv_blk{k}", [2 * G, P]) for k in range(2)]
        prob = [sc.sb(f"prob{k}", [P, NW, SC]) for k in range(2)]
        expd = sc.sb("expd", [P, NW, SC])
        shifted = sc.sb("shifted", [P, NW, SC])
        top = sc.sb("att_top", [P, NW, 4])
        den = sc.sb("att_den", [P, NW, 4])
        rec = sc.sb("att_rec", [P, NW, 4])
        pt_loc = sc.sb("pt_loc", [P, NW, 2, WIN])
        pt_glob = sc.sb("pt_glob", [2 * G, NW, WIN])
        att = sc.sb("att", [P, S])
        mask = sc.sb("mask", [P, 2 * WIN], F32R)
        mask_raw = sc.sb("mask_raw", [P, 2 * WIN])
        ident_r = sc.sb("ident_r", [P, P], F32R)
        head_mask = sc.sb("head_mask", [P, 2 * G])
        head_mask_t = sc.sb("head_mask_t", [2 * G, P])
        pj = [sc.ps(f"pj{k}", [P, S]) for k in range(2)]
        sc_ps = sc.ps("sc_ps", [P, NW, S])
        turn = sc.ps("turn", [P, S])
        o_ps = sc.ps("o_ps", [P, S])
        const_in, x_in = sc.sem("a_const_in"), sc.sem("a_x_in")
        w_raw_in, w_in, wo_in = ([sc.sem(f"a_{n}{k}") for k in range(2)] for n in ("w_raw_in", "w_in", "wo_in"))
        names = ["mask_done", "w_hi_done", "w_split", "q_ready", "k_ready", "v_ready", "g_ready", "q_kept", "k_kept", "v_kept",
                 "gk_kept", "gv_kept", "scored", "top_done", "shift_done", "exp_done", "den_done", "rec_done",
                 "prob_done", "turned", "turn_kept", "mixed", "att_kept", "wo_ready", "acc_done"]
        s = {n: sc.sem(f"a_{n}") for n in names}

        with nc.Block() as block:
            @block.sync
            def _(sp):
                for name, dst in (("mask", mask_raw), ("head_mask", head_mask), ("head_mask_t", head_mask_t)):
                    sp.dma_start(dst[:], dram[name]).then_inc(const_in, 16)
                for hp in range(2):
                    sp.dma_start(w_raw[:, hp], dram["w_qkv"][hp]).then_inc(w_raw_in[hp], 16)
                start(sp, s.values())
                with sp.Fori(0, HP // 2 - 1) as pair:
                    for k in range(2):
                        sp.wait_ge(s["w_split"], START + 2 * pair + k + 1)
                        sp.dma_start(w_raw[:, k], dram["w_qkv"][2 * pair + k + 2]).then_inc(w_raw_in[k], 16)

            @block.scalar
            def _(act):
                act.wait_ge(const_in, 48)
                nc.scalar.copy(mask[:], mask_raw[:]).then_inc(s["mask_done"], 1)
                nc.scalar.copy(ident_r[:], ident[:]).then_inc(s["mask_done"], 1)

            @block.vector
            def _(dve):
                with dve.Fori(0, HP // 2) as pair:
                    for k in range(2):
                        hp = 2 * pair + k
                        dve.wait_ge(w_raw_in[k], 16 * (pair + 1))
                        nc.vector.tensor_copy(w_all[:, hp, 0:3, :], w_raw[:, k]).then_inc(s["w_hi_done"], 1)
                        dve.wait_ge(s["w_hi_done"], START + hp + 1)
                        nc.vector.tensor_tensor(w_all[:, hp, 3:6, :], w_raw[:, k],
                                                w_all[:, hp, 0:3, :].bitcast(F32), ALU.subtract)\
                            .then_inc(s["w_split"], 1)

            @block.gpsimd
            def _(pool):
                for k in range(2):
                    nc.gpsimd.memset(k_blk[k][:], 0.0)
                nc.gpsimd.memset(acc[:], 0.0)

        def at_least(eng, sem, count):
            if not isinstance(count, int) or count > 0:
                eng.wait_ge(s[sem], START + count)

        def units(eng, project, score, mix):
            project(0, 0)
            score(0, 0)
            project(1, 1)
            with eng.Fori(0, U // 2 - 1) as pair:
                for k in range(2):
                    mix(2 * pair + k, k, True)
            mix(U - 2, 0, False)
            mix(U - 1, 1, None)

        with nc.Block() as block:
            @block.sync
            def _(sp):
                def stage_x(b):
                    c = bass.ts(b, S)
                    sp.dma_start(xst[:, 0, :].bitcast(F32), buf["xn_hi"][:, c].bitcast(F32)).then_inc(x_in, 16)
                    sp.dma_start(xst[:, 1, :].bitcast(F32), buf["xn_lo"][:, c].bitcast(F32)).then_inc(x_in, 16)
                    sp.dma_start(xgst[:].bitcast(F32), buf["xg"][:, b].bitcast(F32)).then_inc(x_in, 16)

                def stage_w(hp, k):
                    sp.dma_start(w_st[k][:].bitcast(F32), w_all[:, hp].bitcast(F32)).then_inc(w_in[k], 16)

                def stage_wo(hp, k):
                    sp.dma_start(wo_st[k][:], dram["wo"][hp]).then_inc(wo_in[k], 16)

                stage_x(0)
                stage_w(0, 0)
                stage_w(1, 1)
                stage_wo(0, 0)

                def unit(b, pair, k, hp_before):
                    u = HP * b + 2 * pair + k
                    sp.wait_ge(s["g_ready"], START + u - 1)
                    stage_w(2 * pair + k, k)
                    sp.wait_ge(s["wo_ready"], START + u - 2)
                    stage_wo(hp_before, 1 - k)

                def rest_of_batch(b):
                    with sp.Fori(1, HP // 2) as pair:
                        unit(b, pair, 0, 2 * pair - 1)
                        unit(b, pair, 1, 2 * pair)

                rest_of_batch(0)
                with sp.Fori(1, B) as b:
                    sp.wait_ge(s["g_ready"], START + HP * b)
                    stage_x(b)
                    unit(b, 0, 0, HP - 1)
                    unit(b, 0, 1, 0)
                    rest_of_batch(b)
                sp.wait_ge(s["wo_ready"], START + U - 2)
                stage_wo(HP - 1, 1)

            @block.tensor
            def _(pe):
                def three(out, a_hi, a_lo, b_hi, b_lo):
                    nc.tensor.matmul(out, a_hi, b_hi, start=True, stop=False)
                    nc.tensor.matmul(out, a_hi, b_lo, start=False, stop=False)
                    return nc.tensor.matmul(out, a_lo, b_hi, start=False, stop=True)

                def project_q(u, k):
                    pe.wait_ge(w_in[k], 16 * (u // 2 + 1))
                    pe.wait_ge(x_in, 48 * (u // HP + 1))
                    at_least(pe, "v_kept", u)
                    three(pj[0][:], w_st[k][:, Q], w_st[k][:, 3 + Q], xst[:, 0], xst[:, 1]).then_inc(s["q_ready"], 1)

                def project_k(u, k):
                    at_least(pe, "gv_kept", u)
                    three(pj[1][:], w_st[k][:, K], w_st[k][:, 3 + K], xst[:, 0], xst[:, 1]).then_inc(s["k_ready"], 1)

                def project_v(u, k):
                    pe.wait_ge(s["q_kept"], START + u + 1)
                    for w in range(NW):
                        c = slice(w * WIN, (w + 1) * WIN)
                        last = three(pj[0][:, c], xst[:, 0, c], xst[:, 1, c], w_st[k][:, V], w_st[k][:, 3 + V])
                    last.then_inc(s["v_ready"], 1)

                def project_g(u, k):
                    pe.wait_ge(s["k_kept"], START + 2 * u + 2)
                    three(pj[1][:, 0:2 * G], w_st[k][:, K], w_st[k][:, 3 + K],
                          xgst[:, 0, 0:2 * G], xgst[:, 1, 0:2 * G])
                    three(pj[1][:, P:2 * P], xgst[:, 0], xgst[:, 1], w_st[k][:, V], w_st[k][:, 3 + V])\
                        .then_inc(s["g_ready"], 1)

                def project(u, k):
                    project_q(u, k)
                    project_k(u, k)
                    project_v(u, k)
                    project_g(u, k)

                def score(u, k):
                    pe.wait_ge(s["q_kept"], START + u + 1)
                    pe.wait_ge(s["k_kept"], START + 2 * u + 2)
                    pe.wait_ge(s["gk_kept"], START + u + 1)
                    for w in range(NW):
                        if w % 2 == 0:
                            at_least(pe, "shift_done", 4 * u - 2 + w)
                        nc.tensor.matmul(sc_ps[:, w, 0:SC], q_t[k][:, w * WIN:(w + 1) * WIN], k_blk[k][:, w, :],
                                         start=True, stop=False, skip_group_check=True)
                        last = nc.tensor.matmul(sc_ps[:, w, 0:2 * WIN], ident_r[:], mask[:],
                                                start=False, stop=True, skip_group_check=True)
                        if w % 2 == 1:
                            last.then_inc(s["scored"], 1)

                def turn_local(u, k, half):
                    pe.wait_ge(s["prob_done"], START + 4 * u + 2 * half + 2)
                    if half == 0:
                        at_least(pe, "acc_done", u)
                    else:
                        pe.wait_ge(s["turn_kept"], START + 3 * u + 1)
                    for i in range(4):
                        w, h = 2 * half + i // 2, i % 2
                        last = nc.tensor.transpose(turn[:, i * WIN:(i + 1) * WIN],
                                                   prob[k][:, w, h * WIN:(h + 1) * WIN], ident[:])
                    last.then_inc(s["turned"], 1)

                def turn_global(u, k):
                    pe.wait_ge(s["turn_kept"], START + 3 * u + 2)
                    hold(pe, buf)
                    for w in range(NW):
                        last = nc.tensor.transpose(turn[0:2 * G, w * WIN:(w + 1) * WIN], prob[k][:, w, 2 * WIN:SC],
                                                   ident[:])
                    last.then_inc(s["turned"], 1)

                def mix_values(u, k):
                    pe.wait_ge(s["turn_kept"], START + 3 * u + 3)
                    at_least(pe, "att_kept", u)
                    for w in range(NW):
                        o_w = o_ps[:, w * WIN:(w + 1) * WIN]
                        nc.tensor.matmul(o_w, gv_blk[k][:], pt_glob[:, w, :], start=True, stop=False,
                                         skip_group_check=True)
                        for h in range(2):
                            hd = slice(h * HD, (h + 1) * HD)
                            last = nc.tensor.matmul(o_w[hd], v_sb[k][:, w, hd], pt_loc[:, w, h, :],
                                                    start=False, stop=True, skip_group_check=True)
                    last.then_inc(s["mixed"], 1)

                def project_out(u, k):
                    pe.wait_ge(wo_in[k], 16 * (u // 2 + 1))
                    pe.wait_ge(s["att_kept"], START + u + 1)
                    nc.tensor.matmul(turn[:], wo_st[k][:], att[:], start=True, stop=True).then_inc(s["wo_ready"], 1)

                def mix(u, k, ahead):
                    if ahead is not None:
                        score(u + 1, 1 - k)
                    turn_local(u, k, 0)
                    if ahead:
                        project_q(u + 2, k)
                    turn_local(u, k, 1)
                    if ahead:
                        project_k(u + 2, k)
                    turn_global(u, k)
                    if ahead:
                        project_v(u + 2, k)
                    mix_values(u, k)
                    if ahead:
                        project_g(u + 2, k)
                    project_out(u, k)

                pe.wait_ge(s["mask_done"], START + 2)
                units(pe, project, score, mix)

            @block.scalar
            def _(act):
                def keep_q(u, k):
                    act.wait_ge(s["q_ready"], START + u + 1)
                    at_least(act, "scored", 2 * u - 2)
                    nc.scalar.copy(q_t[k][:], pj[0][:]).then_inc(s["q_kept"], 1)

                def keep_k(u, k):
                    act.wait_ge(s["k_ready"], START + u + 1)
                    for h in range(2):
                        hd = slice(h * HD, (h + 1) * HD)
                        nc.scalar.copy(k_blk[k][hd, :, h * WIN:(h + 1) * WIN],
                                       pj[1][hd].rearrange("p (w c) -> p w c", w=NW)).then_inc(s["k_kept"], 1)

                def keep_v(u, k):
                    act.wait_ge(s["v_ready"], START + u + 1)
                    at_least(act, "mixed", u - 1)
                    nc.scalar.copy(v_sb[k][:], pj[0][:].rearrange("p (w c) -> p w c", w=NW)).then_inc(s["v_kept"], 1)

                def exp(u, half):
                    w = slice(2 * half, 2 * half + 2)
                    act.wait_ge(s["shift_done"], START + 4 * u + 2 * half + 2)
                    at_least(act, "prob_done", 4 * u)
                    nc.scalar.activation(expd[:, w, :], shifted[:, w, :], ACT.Exp, scale=SCALE)\
                        .then_inc(s["exp_done"], 1)

                def keep_turned(u, i):
                    act.wait_ge(s["turned"], START + 3 * u + i + 1)
                    if i == 0:
                        at_least(act, "mixed", u)
                    if i < 2:
                        src, dst = turn[:].rearrange("p (w h q) -> p w h q", w=2, h=2), pt_loc[:, 2 * i:2 * i + 2]
                    else:
                        src, dst = turn[0:2 * G].rearrange("p (w q) -> p w q", w=NW), pt_glob[:]
                    nc.scalar.copy(dst, src).then_inc(s["turn_kept"], 1)

                def project(u, k):
                    keep_q(u, k)
                    keep_k(u, k)
                    keep_v(u, k)

                def score(u, k):
                    exp(u, 0)
                    exp(u, 1)

                def mix(u, k, ahead):
                    if ahead is not None:
                        exp(u + 1, 0)
                    keep_turned(u, 0)
                    if ahead:
                        keep_q(u + 2, k)
                    if ahead is not None:
                        exp(u + 1, 1)
                    keep_turned(u, 1)
                    if ahead:
                        keep_k(u + 2, k)
                    keep_turned(u, 2)
                    if ahead:
                        keep_v(u + 2, k)

                units(act, project, score, mix)

            @block.vector
            def _(dve):
                def parts(half):
                    w = slice(2 * half, 2 * half + 2)
                    for c0, c1, t0 in ((0, 2 * WIN, 0), (2 * WIN, SC, 2)):
                        yield (lambda x: x[:, w, c0:c1].rearrange("p w (h c) -> p w h c", h=2),
                               lambda x: x[:, w, t0:t0 + 2], (c1 - c0) // 2)

                def shift(u, half):
                    dve.wait_ge(s["scored"], START + 2 * u + half + 1)
                    at_least(dve, "shift_done", 4 * u + 2 * half - 2)
                    for cols, stat, n in parts(half):
                        nc.vector.tensor_reduce(stat(top), cols(sc_ps), AX.X, ALU.max).then_inc(s["top_done"], 1)
                    dve.wait_ge(s["top_done"], START + 4 * u + 2 * half + 2)
                    for cols, stat, n in parts(half):
                        nc.vector.tensor_tensor(cols(shifted), cols(sc_ps),
                                                stat(top).unsqueeze(3).broadcast_to([P, 2, 2, n]), ALU.subtract)\
                            .then_inc(s["shift_done"], 1)

                def sums(u, half):
                    dve.wait_ge(s["exp_done"], START + 2 * u + half + 1)
                    at_least(dve, "rec_done", 2 * u + half - 1)
                    for cols, stat, n in parts(half):
                        nc.vector.tensor_reduce(stat(den), cols(expd), AX.X, ALU.add).then_inc(s["den_done"], 1)
                    dve.wait_ge(s["den_done"], START + 4 * u + 2 * half + 2)
                    w = slice(2 * half, 2 * half + 2)
                    nc.vector.reciprocal(rec[:, w, :], den[:, w, :]).then_inc(s["rec_done"], 1)

                def keep_g(u, k):
                    dve.wait_ge(s["g_ready"], START + u + 1)
                    at_least(dve, "scored", 2 * u - 2)
                    at_least(dve, "mixed", u - 1)
                    nc.vector.tensor_tensor(k_blk[k][:, :, 2 * WIN:SC],
                                            pj[1][:, 0:2 * G].unsqueeze(1).broadcast_to([P, NW, 2 * G]),
                                            head_mask[:].unsqueeze(1).broadcast_to([P, NW, 2 * G]), ALU.mult)\
                        .then_inc(s["gk_kept"], 1)
                    nc.vector.tensor_tensor(gv_blk[k][:], pj[1][0:2 * G, P:2 * P], head_mask_t[:], ALU.mult)\
                        .then_inc(s["gv_kept"], 1)

                def keep_att(u):
                    dve.wait_ge(s["mixed"], START + u + 1)
                    at_least(dve, "wo_ready", u)
                    nc.vector.tensor_copy(att[:], o_ps[:]).then_inc(s["att_kept"], 1)

                def add_out(u):
                    dve.wait_ge(s["wo_ready"], START + u + 1)
                    at_least(dve, "acc_done", u)
                    b = u // HP
                    nc.vector.tensor_tensor(acc[:, bass.ts(b, S)], turn[:], acc[:, bass.ts(b, S)], ALU.add)\
                        .then_inc(s["acc_done"], 1)

                def softmax(u, k):
                    shift(u, 0)
                    shift(u, 1)
                    at_least(dve, "prob_done", 4 * u)
                    sums(u, 0)
                    sums(u, 1)

                def mix(u, k, ahead):
                    if ahead is not None:
                        softmax(u + 1, 1 - k)
                    keep_att(u)
                    if ahead:
                        keep_g(u + 2, k)
                    add_out(u)

                units(dve, keep_g, softmax, mix)

            @block.gpsimd
            def _(pool):
                def normalise(u, k):
                    for half in range(2):
                        w = slice(2 * half, 2 * half + 2)
                        pool.wait_ge(s["rec_done"], START + 2 * u + half + 1)
                        if half == 0:
                            at_least(pool, "turned", 3 * u - 3)
                        for c0, c1, t0 in ((0, 2 * WIN, 0), (2 * WIN, SC, 2)):
                            cols = lambda x: x[:, w, c0:c1].rearrange("p w (h c) -> p w h c", h=2)
                            nc.gpsimd.tensor_tensor(cols(prob[k]), cols(expd),
                                                    rec[:, w, t0:t0 + 2].unsqueeze(3)
                                                    .broadcast_to([P, 2, 2, (c1 - c0) // 2]), ALU.mult)\
                                .then_inc(s["prob_done"], 1)

                def mix(u, k, ahead):
                    if ahead is not None:
                        normalise(u + 1, 1 - k)

                units(pool, lambda u, k: None, normalise, mix)


def macaron(nc, dram):
    with ExitStack() as keep:
        def sb(name, shape, dt=F32):
            return keep.enter_context(nc.sbuf_tensor(name, shape, dt))
        buf = {
            "X": sb("X", [P, NT, D]),
            "xn_hi": sb("xn_hi", [D, T], F32R),
            "xn_lo": sb("xn_lo", [D, T], F32R),
            "acc": sb("acc", [D, T]),
            "logits": sb("logits", [P, NT, E]),
            "ident": sb("ident", [P, P]),
            "gate": sb("gate", [D, E]),
            "iota8": sb("iota8", [P, NT, E]),
            "xn_head": sb("xn_head", [CAND, B, D]),
            "xg": sb("xg", [D, B, 2, P], F32R),
        }
        dram["comb"] = nc.dram_tensor("comb", [E, T], F32).ap()
        load_constants(nc, keep, buf, dram)
        norm_stage(nc, keep, buf, dram, "_n0", 0.0, True, False)
        route_stage(nc, keep, buf, dram, "_r0")
        ffn_stage(nc, keep, buf, dram, "_f0")
        norm_stage(nc, keep, buf, dram, "_n1", 0.5, False, True)
        select_stage(nc, keep, buf, dram)
        attention_stage(nc, keep, buf, dram)
        norm_stage(nc, keep, buf, dram, "_n2", 1.0, True, False)
        route_stage(nc, keep, buf, dram, "_r1")
        ffn_stage(nc, keep, buf, dram, "_f1")
        norm_stage(nc, keep, buf, dram, "_n3", 0.5, False, False, out=dram["out"])


def kernel(**inputs):
    import concourse.bacc as bacc
    from concourse.bass_utils import run_bass_kernel_spmd

    a = {n.removeprefix("L0_"): np.asarray(v) for n, v in inputs.items()}
    by_pair = lambda w: w.reshape(D, HP, P)
    w_up = a["ffn_wg"].transpose(0, 2, 1), a["ffn_wu"].transpose(0, 2, 1)
    w_down = a["ffn_wd"].transpose(0, 2, 1).reshape(E, J, P, D).transpose(0, 2, 1, 3).reshape(E, P, I)
    key, query = np.arange(WIN)[None, :], np.arange(WIN)[:, None]
    causal = np.where(key > query, np.float32(-3e38), np.float32(0)).astype(np.float32)
    arrays = {
        "x": a["attn_x"].reshape(T, D),
        "gate": a["ffn_gate_w"].T,
        "w_ffn": np.concatenate([*w_up, w_down], axis=2),
        "w_qkv": np.stack([by_pair(a["attn_wq"]), by_pair(a["attn_wk"]), by_pair(a["attn_wv"])]).transpose(2, 1, 0, 3),
        "wo": a["attn_wo"].reshape(HP, P, D),
        "ws1": a["attn_ws1"], "bs1": a["attn_bs1"], "ws2": a["attn_ws2"], "bs2": a["attn_bs2"],
        "ident": np.eye(P, dtype=np.float32),
        "iota8": np.broadcast_to(np.arange(E, dtype=np.float32), (P, NT, E)),
        "iota_p": np.arange(CAND, dtype=np.float32)[:, None],
        "block_b": np.repeat(np.eye(B, dtype=np.float32)[:, :, None], G, axis=2),
        "mask": np.concatenate([causal, causal], axis=1),
        "head_mask": np.repeat(np.repeat(np.eye(2, dtype=np.float32), HD, axis=0), G, axis=1),
        "head_mask_t": np.repeat(np.repeat(np.eye(2, dtype=np.float32), G, axis=0), HD, axis=1),
    }
    arrays = {n: np.ascontiguousarray(v) for n, v in arrays.items()}
    nc = bacc.Bacc("TRN2", target_bir_lowering=False, num_devices=1)
    dram = {n: nc.dram_tensor(f"in_{n}", v.shape, mybir.dt.from_np(v.dtype), kind="ExternalInput").ap()
            for n, v in arrays.items()}
    dram["out"] = nc.dram_tensor("out_x", [T, D], F32, kind="ExternalOutput").ap()
    macaron(nc, dram)
    r = run_bass_kernel_spmd(nc, [{f"in_{n}": v for n, v in arrays.items()}], core_ids=[0])
    return r.results[0]["out_x"].reshape(B, S, D)
```

```python
import numpy as np
import concourse.bass as bass
from concourse import mybir
from concourse.alu_op_type import AluOpType as ALU
from contextlib import ExitStack

F32 = mybir.dt.float32
F32R = mybir.dt.float32r
U32 = mybir.dt.uint32
ACT = mybir.ActivationFunctionType
AX = mybir.AxisListType

B, S, D = 8, 512, 128
T = B * S
P = 128
NT = T // P
CH = T // S
TPC = S // P
E, I = 8, 512
J = I // P
H, HD = 16, 64
HP = H * HD // P
WIN = 128
NW = S // WIN
G = 32
SH = D // 4
CAND = B + G
SC = 2 * WIN + 2 * G
SLOT_TILES = -(-2 * T // P) + E
WC = 3 * I
EPS = 1e-5
SCALE = 1.0 / HD ** 0.5
TAKEN = float(np.finfo(np.float32).min)
MASKED = float(np.nextafter(np.float32(TAKEN), np.float32(0)))


def hold(eng, buf):
    eng.sem_inc(buf["held"], 1)


START = 1


def start(nc, sems):
    with nc.Block() as block:
        @block.sync
        def _(sp):
            for sem in sems:
                sp.sem_inc(sem, START)


class Step:

    def __init__(self, base, offset=0):
        self.base, self.offset = base, offset

    def after(self, n):
        return Step(self.base, self.offset + n)

    def count(self, per_step, more=0):
        return per_step * self.base + (per_step * self.offset + more + START)

    def wait(self, eng, sem, per_step, more=0):
        count = self.count(per_step, more)
        if not isinstance(count, int) or count > START:
            eng.wait_ge(sem, count)


class Scope:

    def __init__(self, nc):
        self.nc, self.stack, self.own = nc, ExitStack(), []

    def __enter__(self):
        return self

    def __exit__(self, *error):
        if error[0]:
            return
        own = self.own
        with self.nc.Block() as block:
            @block.gpsimd
            def _(pool):
                for sem in own:
                    pool.sem_clear(sem)
        self.stack.close()

    def sb(self, name, shape, dt=F32):
        return self.stack.enter_context(self.nc.sbuf_tensor(name, shape, dt))

    def ps(self, name, shape, dt=F32):
        return self.stack.enter_context(self.nc.psum_tensor(name, shape, dt))

    def sem(self, name):
        self.own.append(self.stack.enter_context(self.nc.semaphore(name)))
        return self.own[-1]


def load_constants(nc, sems, buf, dram):
    loaded = sems.enter_context(nc.semaphore("start_loaded"))
    buf["held"] = sems.enter_context(nc.semaphore("held"))
    with nc.Block() as block:
        @block.sync
        def _(sp):
            sp.dma_start(buf["X"][:], dram["x"].rearrange("(t p) d -> p t d", p=P)).then_inc(loaded, 16)
            sp.dma_start(buf["ident"][:], dram["ident"]).then_inc(loaded, 16)
            sp.dma_start(buf["gate"][:], dram["gate"]).then_inc(loaded, 16)
            sp.dma_start(buf["iota8"][:], dram["iota8"]).then_inc(loaded, 16)
            sp.wait_ge(loaded, 64)


def norm_stage(nc, buf, dram, tag, source, use):
    sc = Scope(nc)
    X, acc, ident = buf["X"], buf["acc"], buf["ident"]
    UPDATES = TPC if source == "pairs" else 1
    norm, route, attend = use != "store", use == "route", use == "attend"
    with sc:
        x_norm = [sc.sb(f"x_norm{k}{tag}", [P, TPC, D]) for k in range(2)]
        stats = [sc.sb(f"stats{k}{tag}", [P, TPC, 6]) for k in range(2)]
        mean_var = [sc.sb(f"mean_var{k}{tag}", [P, TPC, 2]) for k in range(2)]
        std = [sc.sb(f"std{k}{tag}", [P, TPC]) for k in range(2)]
        rstd = [sc.sb(f"rstd{k}{tag}", [P, TPC]) for k in range(2)]
        xnt = [sc.sb(f"xnt{k}{tag}", [P, S]) for k in range(2)]
        incoming = [sc.sb(f"incoming{k}{tag}", [P, 2 * S]) for k in range(2)]
        eps = sc.sb(f"eps{tag}", [P, 1])
        acc_tok = [sc.ps(f"acc_tok{k}{tag}", [P, TPC, D]) for k in range(2)]
        xnt_ps = [sc.ps(f"xnt_ps{k}{tag}", [P, S]) for k in range(2)]
        lg_ps = [sc.ps(f"lg_ps{k}{tag}", [P, TPC, E]) for k in range(2)]
        names = ["acc_staged", "acc_turned", "half_added", "x_updated", "stats_done", "aggr_done",
                 "std_done", "rstd_done", "normed", "turned", "hi_done", "lo_done", "xnt_done", "logits_done",
                 "logits_kept", "eps_set", "head_kept"]
        s = {n: sc.sem(f"{n}{tag}") for n in names}
        stored = [sc.sem(f"stored{k}{tag}") for k in range(2)]
        pairs_in = [sc.sem(f"pairs_in{k}{tag}") for k in range(2)]
        pair_of = [incoming[k][:].rearrange("p (t j d) -> p t j d", t=TPC, j=2) for k in range(2)]

        def chunks(eng, first, second):
            first(Step(0), 0)
            with eng.Fori(0, CH - 3, 2) as c:
                for k in range(2):
                    first(Step(c, k + 1), 1 - k)
                    second(Step(c, k), k)
            first(Step(CH - 1), 1)
            second(Step(CH - 2), 0)
            second(Step(CH - 1), 1)

        def index(c):
            return c.base + c.offset

        start(nc, s.values())
        with nc.Block() as block:
            @block.sync
            def _(sp):
                row_tiles = (dram["xn"] if norm else dram["out"]).rearrange("(c t p) d -> c p t d", p=P, t=TPC)

                def store(c, k):
                    if route:
                        sp.wait_ge(s["normed"], c.count(TPC, TPC))
                        sp.dma_start(row_tiles[index(c)], x_norm[k][:]).then_inc(stored[k], 16)
                    elif not norm:
                        sp.wait_ge(s["x_updated"], c.count(UPDATES, UPDATES))
                        sp.dma_start(row_tiles[index(c)], X[:, bass.ts(index(c), TPC), :]).then_inc(stored[k], 16)

                chunks(sp, lambda c, k: None, store)
                if route or not norm:
                    for k in range(2):
                        sp.wait_ge(stored[k], 16 * CH // 2)

            @block.gpsimd
            def _(pool):
                def bring(c, k):
                    if source == "acc":
                        c.wait(pool, s["acc_turned"], 1, -1)
                        hold(pool, buf)
                        nc.gpsimd.tensor_copy(incoming[k][:, 0:S], acc[:, bass.ts(index(c), S)])\
                            .then_inc(s["acc_staged"], 1)

                if source == "pairs":
                    for c in range(CH):
                        if c >= 2:
                            pool.wait_ge(s["x_updated"], START + UPDATES * (c - 1))
                        for t in range(TPC):
                            for j in range(2):
                                nc.gpsimd.indirect_dma_start(
                                    pair_of[c % 2][:, t, j, :], None, dram["y"],
                                    bass.IndirectOffsetOnAxis(ap=buf["slot"][:, c * TPC + t, j:j + 1], axis=0))\
                                    .then_inc(pairs_in[c % 2], 16)
                chunks(pool, bring, lambda c, k: None)

            @block.tensor
            def _(pe):
                def turn_acc(c, k):
                    if source == "acc":
                        pe.wait_ge(s["acc_staged"], c.count(1, 1))
                        c.wait(pe, s["x_updated"], 1, -1)
                        for t in range(TPC):
                            last = nc.tensor.transpose(acc_tok[k][:, t, :], incoming[k][:, t * P:(t + 1) * P],
                                                       ident[:])
                        last.then_inc(s["acc_turned"], 1)

                def turn(c, k):
                    if not norm:
                        return
                    pe.wait_ge(s["normed"], c.count(TPC, TPC))
                    c.wait(pe, s["lo_done" if attend else "xnt_done"], 1, -1)
                    for t in range(TPC):
                        last = nc.tensor.transpose(xnt_ps[k][:, t * P:(t + 1) * P], x_norm[k][:, t, :], ident[:])
                    last.then_inc(s["turned"], 1)
                    if route:
                        pe.wait_ge(s["xnt_done"], c.count(1, 1))
                        c.wait(pe, s["logits_kept"], 1, -1)
                        for t in range(TPC):
                            last = nc.tensor.matmul(lg_ps[k][:, t, :], xnt[k][:, t * P:(t + 1) * P], buf["gate"][:],
                                                    start=True, stop=True)
                        last.then_inc(s["logits_done"], 1)

                chunks(pe, turn_acc, turn)

            @block.scalar
            def _(act):
                def root(c, k):
                    if norm:
                        act.wait_ge(s["aggr_done"], c.count(TPC, TPC))
                        c.wait(act, s["rstd_done"], 1, -1)
                        nc.scalar.activation(std[k][:], mean_var[k][:, :, 1], ACT.Sqrt, bias=eps[:])\
                            .then_inc(s["std_done"], 1)

                def keep(c, k):
                    if norm:
                        act.wait_ge(s["turned"], c.count(1, 1))
                    if attend:
                        nc.scalar.copy(buf["xn_hi"][:, bass.ts(index(c), S)], xnt_ps[k][:]).then_inc(s["hi_done"], 1)
                    if route:
                        c.wait(act, s["logits_done"], 1, -1)
                        nc.scalar.copy(xnt[k][:], xnt_ps[k][:]).then_inc(s["xnt_done"], 1)

                if norm:
                    act.wait_ge(s["eps_set"], START + 1)
                chunks(act, root, keep)

            @block.vector
            def _(dve):
                def update(c, k):
                    x_c = X[:, bass.ts(index(c), TPC), :]
                    if source == "acc":
                        dve.wait_ge(s["acc_turned"], c.count(1, 1))
                        nc.vector.tensor_tensor(x_c, acc_tok[k][:], x_c, ALU.add).then_inc(s["x_updated"], 1)
                    if source == "pairs":
                        dve.wait_ge(pairs_in[k], 128 // 2 * c.base + (128 // 2 * (c.offset - k) + 128))
                        for j in range(2):
                            if j:
                                dve.wait_ge(s["half_added"], c.count(TPC, TPC))
                            for t in range(TPC):
                                at = index(c) * TPC + t
                                nc.vector.scalar_tensor_tensor(
                                    X[:, at, :], pair_of[k][:, t, j, :], buf["weight"][:, at, j:j + 1],
                                    X[:, at, :], ALU.mult, ALU.add).then_inc(s["x_updated" if j else "half_added"], 1)
                    if norm:
                        if source:
                            dve.wait_ge(s["x_updated"], c.count(UPDATES, UPDATES))
                        c.wait(dve, s["normed"], TPC, -TPC)
                        hold(dve, buf)
                        for t in range(TPC):
                            nc.vector.bn_stats(stats[k][:, t, :], X[:, index(c) * TPC + t, :])\
                                .then_inc(s["stats_done"], 1)
                        dve.wait_ge(s["stats_done"], c.count(TPC, TPC))
                        hold(dve, buf)
                        for t in range(TPC):
                            nc.vector.bn_aggr(mean_var[k][:, t, :], stats[k][:, t, :]).then_inc(s["aggr_done"], 1)

                def normalise(c, k):
                    if not norm:
                        return
                    dve.wait_ge(s["std_done"], c.count(1, 1))
                    nc.vector.reciprocal(rstd[k][:], std[k][:]).then_inc(s["rstd_done"], 1)
                    dve.wait_ge(s["rstd_done"], c.count(1, 1))
                    c.wait(dve, s["turned"], 1, -1)
                    if route and (not isinstance(c.base, int) or index(c) >= 2):
                        dve.wait_ge(stored[k], 8 * (c.base + (c.offset - k)))
                    for t in range(TPC):
                        nc.vector.tensor_scalar(x_norm[k][:, t, :], X[:, index(c) * TPC + t, :],
                                                mean_var[k][:, t, 0:1], rstd[k][:, t:t + 1],
                                                ALU.subtract, ALU.mult).then_inc(s["normed"], 1)
                    if attend:
                        dve.wait_ge(s["normed"], c.count(TPC, 1))
                        nc.vector.tensor_copy(buf["xn_head"][:, index(c), :], x_norm[k][0:CAND, 0, :])
                        dve.wait_ge(s["hi_done"], c.count(1, 1))
                        xn = bass.ts(index(c), S)
                        nc.vector.tensor_tensor(buf["xn_lo"][:, xn], xnt_ps[k][:], buf["xn_hi"][:, xn].bitcast(F32),
                                                ALU.subtract).then_inc(s["lo_done"], 1)
                    if route:
                        dve.wait_ge(s["logits_done"], c.count(1, 1))
                        nc.vector.tensor_copy(buf["logits"][:, bass.ts(index(c), TPC), :], lg_ps[k][:])\
                            .then_inc(s["logits_kept"], 1)

                if norm:
                    nc.vector.memset(eps[:], EPS).then_inc(s["eps_set"], 1)
                chunks(dve, update, normalise)


def route_stage(nc, buf, dram, tag):
    sc = Scope(nc)
    logits, w_hi, w_lo = buf["logits"], buf["w_hi"], buf["w_lo"]
    NS = SLOT_TILES
    with sc:
        stage = [sc.sb(f"w_stage{k}{tag}", [P, WC]) for k in range(2)]
        top = sc.sb(f"top{tag}", [P, NT, 8])
        top_i = sc.sb(f"top_i{tag}", [P, NT, 8], U32)
        pick = sc.sb(f"pick{tag}", [P, NT, 2])
        diff = sc.sb(f"diff{tag}", [P, NT])
        e2 = sc.sb(f"e2{tag}", [P, NT])
        den = sc.sb(f"den{tag}", [P, NT])
        soft = sc.sb(f"soft{tag}", [P, NT, 2])
        oh = sc.sb(f"oh{tag}", [P, NT, 2, E])
        member = sc.sb(f"member{tag}", [P, NT, E])
        count = [sc.sb(f"count{k}{tag}", [P, NT, E]) for k in range(2)]
        before = sc.sb(f"before{tag}", [P, NT, E])
        padded = sc.sb(f"padded{tag}", [P, E])
        padded_i = sc.sb(f"padded_i{tag}", [P, E], U32)
        tiles_i = sc.sb(f"tiles_i{tag}", [P, E], U32)
        tiles = sc.sb(f"tiles{tag}", [P, E])
        end = [sc.sb(f"end{k}{tag}", [P, E]) for k in range(2)]
        base = sc.sb(f"base{tag}", [P, E])
        where = sc.sb(f"where{tag}", [P, NT, 2, E])
        slot = sc.sb(f"slot{tag}", [P, NT, 2])
        tile_i = sc.sb(f"tile_i{tag}", [P, NT, 2], U32)
        tile_f = sc.sb(f"tile_f{tag}", [P, NT, 2])
        lane = sc.sb(f"lane{tag}", [P, NT, 2])
        past = sc.sb(f"past{tag}", [1, NS, E])
        owner = sc.sb(f"owner{tag}", [1, NS])
        R = 4
        in_lane = sc.sb(f"in_lane{tag}", [P, R, P], F32R)
        in_tile = sc.sb(f"in_tile{tag}", [P, R, NS], F32R)
        rank_ps = sc.ps(f"rank_ps{tag}", [P, NT, E])
        count_ps = sc.ps(f"count_ps{tag}", [P, NT, E])
        table_ps = sc.ps(f"table_ps{tag}", [P, NS])
        w_in = [sc.sem(f"w_in{k}{tag}") for k in range(2)]
        names = ["w_hi_done", "w_lo_done", "placed", "tabled"]
        s = {n: sc.sem(f"r_{n}{tag}") for n in names}
        consts_in, chain, e2_done, member_done, counted, cleared = (
            sc.sem(f"r_{n}{tag}") for n in ("consts_in", "chain", "e2_done", "member_done", "counted", "cleared"))
        c_lower = sc.sb(f"lower{tag}", [P, P])
        c_ones = sc.sb(f"ones{tag}", [P, P])
        c_iota = sc.sb(f"iota{tag}", [P, P])
        c_token = sc.sb(f"token{tag}", [P, NT])
        c_tile = sc.sb(f"tile_iota{tag}", [1, NS, E])
        zero = sc.sb(f"zero{tag}", [P, P], F32R)
        consts = ((c_lower, "lower"), (c_ones, "ones"), (c_iota, "iota_row"), (c_token, "token"),
                  (c_tile, "iota_tile"))
        start(nc, s.values())
        with nc.Block() as block:
            @block.sync
            def _(sp):
                for k in range(2):
                    sp.dma_start(stage[k][:], dram["w_ffn"][k]).then_inc(w_in[k], 16)
                for dst, name in consts:
                    sp.dma_start(dst[:], dram[name]).then_inc(consts_in, 16)
                with sp.Fori(0, E - 3, 2) as e:
                    for k in range(2):
                        sp.wait_ge(s["w_lo_done"], Step(e, k).count(1, 1))
                        sp.dma_start(stage[k][:], dram["w_ffn"][e + (k + 2)]).then_inc(w_in[k], 16)

            @block.scalar
            def _(act):
                def split_hi(e, k):
                    act.wait_ge(w_in[k], 8 * e.base + (8 * (e.offset - k) + 16))
                    nc.scalar.copy(w_hi[:, bass.ts(e.base + e.offset, WC)], stage[k][:]).then_inc(s["w_hi_done"], 1)

                for e in range(2):
                    split_hi(Step(e), e)
                act.wait_ge(chain, 2 * NT + 1)
                nc.scalar.activation(e2[:], diff[:], ACT.Exp).then_inc(e2_done, 1)
                with act.Fori(2, E - 1, 2) as e:
                    for k in range(2):
                        split_hi(Step(e, k), k)

            @block.gpsimd
            def _(pool):
                with pool.Fori(0, E - 1, 2) as e:
                    for k in range(2):
                        pool.wait_ge(s["w_hi_done"], Step(e, k).count(1, 1))
                        w = bass.ts(e + k, WC)
                        nc.gpsimd.tensor_tensor(w_lo[:, w], stage[k][:], w_hi[:, w].bitcast(F32), ALU.subtract)\
                            .then_inc(s["w_lo_done"], 1)

            @block.tensor
            def _(pe):
                pe.wait_ge(consts_in, 16 * len(consts))
                pe.wait_ge(member_done, 1)
                nc.tensor.matmul(rank_ps[:], c_lower[:], member[:], start=True, stop=True)
                nc.tensor.matmul(count_ps[:], c_ones[:], member[:], start=True, stop=True).then_inc(counted, 1)
                pe.wait_ge(cleared, 1)
                nc.tensor.matmul(table_ps[:], in_lane[:, 0, :], zero[:, 0:NS], start=True, stop=False, skip_group_check=True)\
                    .then_inc(s["tabled"], R)
                with pe.Fori(0, 2 * NT - R + 1, R) as q:
                    for r in range(R):
                        pe.wait_ge(s["placed"], Step(q, r).count(2, 2))
                        nc.tensor.matmul(table_ps[:], in_lane[:, r, :], in_tile[:, r], start=False, stop=True,
                                         skip_group_check=True).then_inc(s["tabled"], 1)

            @block.vector
            def _(dve):
                n = [0]

                def step(ins):
                    n[0] += 1
                    ins.then_inc(chain, 1)

                def settled():
                    dve.wait_ge(chain, n[0])

                v = nc.vector
                for t in range(NT):
                    step(v.max(top[:, t, :], logits[:, t, :]))
                settled()
                for t in range(NT):
                    step(v.max_index(top_i[:, t, :], top[:, t, :], logits[:, t, :]))
                step(v.tensor_tensor(diff[:], top[:, :, 1], top[:, :, 0], ALU.subtract))
                settled()
                step(v.tensor_copy(pick[:], top_i[:, :, 0:2]))
                settled()
                for k in range(2):
                    step(v.tensor_tensor(oh[:, :, k, :], buf["iota8"][:],
                                         pick[:, :, k:k + 1].broadcast_to([P, NT, E]), ALU.is_equal))
                step(v.memset(zero[:].bitcast(F32), 0.0))
                settled()
                v.tensor_tensor(member[:], oh[:, :, 0, :], oh[:, :, 1, :], ALU.add).then_inc(member_done, 1)
                v.tensor_copy(in_lane[:, 0, :], zero[:].bitcast(F32)).then_inc(cleared, 1)
                dve.wait_ge(e2_done, 1)
                step(v.tensor_scalar_add(den[:], e2[:], 1.0))
                settled()
                step(v.reciprocal(soft[:, :, 0], den[:]))
                settled()
                step(v.tensor_tensor(soft[:, :, 1], e2[:], soft[:, :, 0], ALU.mult))
                settled()
                step(v.tensor_scalar(buf["weight"][:], soft[:], 0.5, None, ALU.mult))
                dve.wait_ge(counted, 1)
                step(v.tensor_copy(count[0][:], count_ps[:]))
                settled()
                src, d = 0, 1
                while d < NT:
                    step(v.tensor_copy(count[1 - src][:, 0:d, :], count[src][:, 0:d, :]))
                    step(v.tensor_tensor(count[1 - src][:, d:, :], count[src][:, d:, :], count[src][:, :-d, :], ALU.add))
                    settled()
                    src, d = 1 - src, 2 * d
                total = count[src]
                step(v.tensor_tensor(before[:], total[:], count_ps[:], ALU.subtract))
                step(v.tensor_scalar_add(padded[:], total[:, NT - 1, :], float(P - 1)))
                settled()
                step(v.tensor_tensor(before[:], rank_ps[:], before[:], ALU.add))
                step(v.tensor_copy(padded_i[:], padded[:]))
                settled()
                step(v.tensor_scalar(tiles_i[:], padded_i[:], P.bit_length() - 1, None, ALU.logical_shift_right))
                settled()
                step(v.tensor_copy(tiles[:], tiles_i[:]))
                settled()
                step(v.tensor_copy(end[0][:], tiles[:]))
                settled()
                src, d = 0, 1
                while d < E:
                    step(v.tensor_copy(end[1 - src][:, 0:d], end[src][:, 0:d]))
                    step(v.tensor_tensor(end[1 - src][:, d:], end[src][:, d:], end[src][:, :-d], ALU.add))
                    settled()
                    src, d = 1 - src, 2 * d
                ends = end[src]
                step(v.tensor_tensor(base[:], ends[:], tiles[:], ALU.subtract))
                dve.wait_ge(consts_in, 16 * len(consts))
                step(v.tensor_tensor(past[:], c_tile[:], ends[0:1].unsqueeze(1).broadcast_to([1, NS, E]), ALU.is_ge))
                settled()
                step(v.tensor_scalar(base[:], base[:], float(P), None, ALU.mult))
                step(v.tensor_reduce(owner[:], past[:], AX.X, ALU.add))
                settled()
                step(v.tensor_scalar(buf["owner"][:], owner[:], float(E - 1), float(WC), ALU.min, ALU.mult))
                step(v.tensor_tensor(before[:], before[:], base[:].unsqueeze(1).broadcast_to([P, NT, E]), ALU.add))
                settled()
                step(v.tensor_tensor(where[:], oh[:], before[:].unsqueeze(2).broadcast_to([P, NT, 2, E]), ALU.mult))
                settled()
                step(v.tensor_reduce(slot[:], where[:], AX.X, ALU.add))
                settled()
                step(v.tensor_copy(buf["slot"][:], slot[:]))
                settled()
                step(v.tensor_scalar(tile_i[:], buf["slot"][:], P.bit_length() - 1, None, ALU.logical_shift_right))
                settled()
                step(v.tensor_copy(tile_f[:], tile_i[:]))
                settled()
                step(v.scalar_tensor_tensor(lane[:], tile_f[:], float(-P), slot[:], ALU.mult, ALU.add))
                settled()
                with dve.Fori(0, NT - R // 2 + 1, R // 2) as t:
                    for r in range(R):
                        q = Step(t, r // 2)
                        dve.wait_ge(s["tabled"], q.count(2, r % 2 + 1))
                        at = t + r // 2
                        tile_of, lane_of = tile_f[:, at, r % 2:r % 2 + 1], lane[:, at, r % 2:r % 2 + 1]
                        v.tensor_scalar(in_lane[:, r, :], c_iota[:], lane_of, None, ALU.is_equal)\
                            .then_inc(s["placed"], 1)
                        v.tensor_scalar(in_tile[:, r, :], c_iota[:, 0:NS], tile_of, c_token[:, bass.ds(at, 1)],
                                        ALU.is_equal, ALU.mult).then_inc(s["placed"], 1)
                dve.wait_ge(s["tabled"], START + R + 2 * NT)
                step(v.tensor_copy(buf["row_in"][:], table_ps[:]))


def ffn_stage(nc, buf, dram, tag):
    sc = Scope(nc)
    ident, w_hi, w_lo = buf["ident"], buf["w_hi"], buf["w_lo"]
    NS = SLOT_TILES
    M = 4
    with sc:
        x_in = [sc.sb(f"x_in{m}{tag}", [P, D]) for m in range(M)]
        xt_hi = [sc.sb(f"xt_hi{k}{tag}", [D, P], F32R) for k in range(2)]
        xt_lo = [sc.sb(f"xt_lo{k}{tag}", [D, P], F32R) for k in range(2)]
        silu = [sc.sb(f"silu{k}{tag}", [P, I]) for k in range(2)]
        hid = [sc.sb(f"hid{k}{tag}", [P, I]) for k in range(2)]
        ht_hi = [sc.sb(f"ht_hi{k}{tag}", [P, J, P], F32R) for k in range(2)]
        ht_lo = [sc.sb(f"ht_lo{k}{tag}", [P, J, P], F32R) for k in range(2)]
        y_out = [sc.sb(f"y_out{m}{tag}", [P, D]) for m in range(M)]
        gate_ps = [sc.ps(f"gate_ps{k}{tag}", [P, I]) for k in range(2)]
        up_ps = [sc.ps(f"up_ps{k}{tag}", [P, I]) for k in range(2)]
        xt_ps = sc.ps(f"xt_ps{tag}", [D, P])
        ht_ps = sc.ps(f"ht_ps{tag}", [P, J, P])
        y_ps = [sc.ps(f"y_ps{k}{tag}", [P, D]) for k in range(2)]
        gathered = [sc.sem(f"gathered{m}{tag}") for m in range(M)]
        stored = [sc.sem(f"y_stored{m}{tag}") for m in range(M)]
        names = ["x_turned", "x_hi_done", "x_lo_done", "gate_ready", "up_ready", "silu_done", "hid_done", "h_turned",
                 "h_hi_done", "h_lo_done", "y_ready", "y_kept"]
        s = {n: sc.sem(f"f_{n}{tag}") for n in names}

        def tiles(eng, make, turn_h, finish, turn_x):
            turn_x(Step(0), 0)
            turn_x(Step(1), 1)
            make(Step(0), 0)

            def step(i, m, first=False, left=3):
                if left > 1:
                    make(i.after(1), (m + 1) % M)
                if left > 2:
                    turn_x(i.after(2), (m + 2) % M)
                turn_h(i, m)
                if not first:
                    finish(i.after(-1), (m - 1) % M)

            step(Step(0), 0, first=True)
            with eng.Fori(0, NS - 2 * M + 1, M) as i:
                for m in range(1, M + 1):
                    step(Step(i, m), m % M)
            for left in range(M - 1, 0, -1):
                step(Step(NS - left), M - left, left=left)
            finish(Step(NS - 1), M - 1)

        def nothing(i, m):
            pass

        start(nc, s.values())
        with nc.Block() as block:
            @block.sync
            def _(sp):
                rows = dram["y"].rearrange("(i p) d -> i p d", p=P)

                def store(i, m):
                    sp.wait_ge(s["y_kept"], i.count(1, 1))
                    sp.dma_start(rows[i.base + i.offset], y_out[m][:]).then_inc(stored[m], 16)

                tiles(sp, nothing, nothing, store, nothing)
                for m in range(M):
                    sp.wait_ge(stored[m], 16 * NS // M)

            @block.gpsimd
            def _(pool):
                for i in range(NS):
                    if i >= M:
                        pool.wait_ge(s["x_turned"], START + i - M + 1)
                    nc.gpsimd.indirect_dma_start(
                        x_in[i % M][:], None, dram["xn"],
                        bass.IndirectOffsetOnAxis(ap=buf["row_in"][:, i:i + 1], axis=0)).then_inc(gathered[i % M], 16)

            @block.tensor
            def _(pe):
                kept = [pe.alloc_register(f"weights{m}{tag}") for m in range(M)]

                def turn_x(i, m):
                    pe.wait_ge(gathered[m], 4 * i.base + (4 * (i.offset - m) + 16))
                    i.wait(pe, s["x_lo_done"], 1)
                    nc.tensor.transpose(xt_ps[:], x_in[m][:], ident[:]).then_inc(s["x_turned"], 1)

                def make(i, m):
                    k = m % 2
                    at = pe.value_load(buf["owner"][0:1, bass.ds(i.base + i.offset, 1)])
                    at = at.with_bounds(min_val=0, max_val=(E - 1) * WC)
                    pe.reg_mov(kept[m], at)
                    pe.wait_ge(s["x_lo_done"], i.count(1, 1))
                    i.wait(pe, s["hid_done"], 1, -1)
                    for n, (out, ready) in enumerate(((gate_ps[k], "gate_ready"), (up_ps[k], "up_ready"))):
                        w = bass.ds(at + n * I, I)
                        nc.tensor.matmul(out[:], xt_hi[k][:], w_hi[:, w], start=True, stop=False)
                        nc.tensor.matmul(out[:], xt_hi[k][:], w_lo[:, w], start=False, stop=False)
                        nc.tensor.matmul(out[:], xt_lo[k][:], w_hi[:, w], start=False, stop=True)\
                            .then_inc(s[ready], 1)

                def turn_h(i, m):
                    pe.wait_ge(s["hid_done"], i.count(1, 1))
                    i.wait(pe, s["h_lo_done"], 1)
                    for j in range(J):
                        last = nc.tensor.transpose(ht_ps[:, j, :], hid[m % 2][:, j * P:(j + 1) * P], ident[:])
                    last.then_inc(s["h_turned"], 1)

                def finish(i, m):
                    k = m % 2
                    at = bass.RuntimeValue.of_register_unchecked(kept[m]).with_bounds(min_val=0, max_val=(E - 1) * WC)
                    pe.wait_ge(s["h_lo_done"], i.count(1, 1))
                    i.wait(pe, s["y_kept"], 1, -1)
                    for j in range(J):
                        w = bass.ds(at + (2 * I + j * P), P)
                        nc.tensor.matmul(y_ps[k][:], ht_hi[k][:, j, :], w_hi[:, w], start=j == 0, stop=False)
                        nc.tensor.matmul(y_ps[k][:], ht_hi[k][:, j, :], w_lo[:, w], start=False, stop=False)
                        last = nc.tensor.matmul(y_ps[k][:], ht_lo[k][:, j, :], w_hi[:, w],
                                                start=False, stop=j == J - 1)
                    last.then_inc(s["y_ready"], 1)

                tiles(pe, make, turn_h, finish, turn_x)

            @block.scalar
            def _(act):
                def turn_x(i, m):
                    act.wait_ge(s["x_turned"], i.count(1, 1))
                    i.wait(act, s["up_ready"], 1, -1)
                    nc.scalar.copy(xt_hi[m % 2][:], xt_ps[:]).then_inc(s["x_hi_done"], 1)

                def make(i, m):
                    act.wait_ge(s["gate_ready"], i.count(1, 1))
                    i.wait(act, s["hid_done"], 1, -1)
                    nc.scalar.activation(silu[m % 2][:], gate_ps[m % 2][:], ACT.Silu).then_inc(s["silu_done"], 1)

                def turn_h(i, m):
                    act.wait_ge(s["h_turned"], i.count(1, 1))
                    i.wait(act, s["y_ready"], 1, -1)
                    nc.scalar.copy(ht_hi[m % 2][:], ht_ps[:]).then_inc(s["h_hi_done"], 1)

                tiles(act, make, turn_h, nothing, turn_x)

            @block.vector
            def _(dve):
                def turn_x(i, m):
                    dve.wait_ge(s["x_hi_done"], i.count(1, 1))
                    nc.vector.tensor_tensor(xt_lo[m % 2][:], xt_ps[:], xt_hi[m % 2][:].bitcast(F32), ALU.subtract)\
                        .then_inc(s["x_lo_done"], 1)

                def make(i, m):
                    dve.wait_ge(s["silu_done"], i.count(1, 1))
                    dve.wait_ge(s["up_ready"], i.count(1, 1))
                    i.wait(dve, s["h_turned"], 1, -1)
                    nc.vector.tensor_tensor(hid[m % 2][:], up_ps[m % 2][:], silu[m % 2][:], ALU.mult)\
                        .then_inc(s["hid_done"], 1)

                def turn_h(i, m):
                    dve.wait_ge(s["h_hi_done"], i.count(1, 1))
                    nc.vector.tensor_tensor(ht_lo[m % 2][:], ht_ps[:], ht_hi[m % 2][:].bitcast(F32), ALU.subtract)\
                        .then_inc(s["h_lo_done"], 1)

                def finish(i, m):
                    dve.wait_ge(s["y_ready"], i.count(1, 1))
                    if not isinstance(i.base, int) or i.offset + i.base >= M:
                        dve.wait_ge(stored[m], 4 * i.base + 4 * (i.offset - m))
                    nc.vector.tensor_copy(y_out[m][:], y_ps[m % 2][:]).then_inc(s["y_kept"], 1)

                tiles(dve, make, turn_h, finish, turn_x)


def select_stage(nc, buf, dram):
    sc = Scope(nc)
    with sc:
        ws1 = sc.sb("ws1", [D, SH])
        bs1 = sc.sb("bs1", [SH, 1])
        ws2 = sc.sb("ws2", [SH, 1])
        bs2 = sc.sb("bs2", [B, 1])
        iota_p = sc.sb("iota_p", [CAND, 1])
        block_b = sc.sb("block_b", [B, B, G])
        xs = sc.sb("xs", [D, B, B])
        hid = sc.sb("sel_hid", [SH, B, B])
        raw = sc.sb("raw", [B, B])
        score = sc.sb("score", [B, 4, CAND])
        best = sc.sb("best", [B, G])
        best_i = sc.sb("best_i", [B, G], U32)
        best_f = sc.sb("best_f", [B, G])
        wide = sc.sb("wide", [B, B, G])
        ones = sc.sb("ones", [B, CAND])
        onehot = sc.sb("onehot", [CAND, B, G])
        hid_ps = sc.ps("sel_hid_ps", [SH, B * B])
        score_ps = sc.ps("score_ps", [B, B])
        idx_ps = sc.ps("idx_ps", [CAND, B * G])
        xg_ps = sc.ps("xg_ps", [D, B, G])
        xg = buf["xg"]
        v_chain, loaded, xs_done, hid_ready, gelu_done, score_ready, masked, wide_done, idx_ready, onehot_done, \
            xg_ready, xg_hi_done, xg_done = (sc.sem(f"sel_{n}") for n in (
                "v_chain", "loaded", "xs_done", "hid_ready", "gelu_done", "score_ready", "masked", "wide_done",
                "idx_ready", "onehot_done", "xg_ready", "xg_hi_done", "xg_done"))
        raw_done = sc.sem("sel_raw_done")
        with nc.Block() as block:
            @block.sync
            def _(sp):
                sp.dma_start(ws1[:], dram["ws1"]).then_inc(loaded, 16)
                sp.dma_start(bs1[:], dram["bs1"].unsqueeze(1)).then_inc(loaded, 16)
                sp.dma_start(ws2[:], dram["ws2"]).then_inc(loaded, 16)
                sp.dma_start(bs2[:], dram["bs2"].partition_broadcast(B)).then_inc(loaded, 16)
                sp.dma_start(iota_p[:], dram["iota_p"]).then_inc(loaded, 16)
                sp.dma_start(block_b[:], dram["block_b"]).then_inc(loaded, 16)

            @block.gpsimd
            def _(pool):
                pool.wait_ge(raw_done, 1)
                nc.gpsimd.affine_select(out=score[:, 0, 0:B], in_=raw[:], pattern=[[-1, B]], compare_op=ALU.is_ge,
                                        fill=MASKED, base=0, channel_multiplier=1).then_inc(masked, 1)

            @block.tensor
            def _(pe):
                pe.wait_ge(loaded, 96)
                pe.wait_ge(xs_done, 1)
                nc.tensor.matmul(hid_ps[:], ws1[:], xs[:], start=True, stop=True).then_inc(hid_ready, 1)
                pe.wait_ge(gelu_done, 1)
                for j in range(B):
                    last = nc.tensor.matmul(score_ps[:, j:j + 1], hid[:, :, j], ws2[:], start=True, stop=True)
                last.then_inc(score_ready, 1)
                pe.wait_ge(wide_done, 1)
                nc.tensor.matmul(idx_ps[:], ones[:], wide[:], start=True, stop=True).then_inc(idx_ready, 1)
                pe.wait_ge(onehot_done, 1)
                for b in range(B):
                    last = nc.tensor.matmul(xg_ps[:, b, :], buf["xn_head"][:, b, :], onehot[:, b, :],
                                            start=True, stop=True)
                last.then_inc(xg_ready, 1)

            @block.scalar
            def _(act):
                act.wait_ge(hid_ready, 1)
                act.wait_ge(loaded, 96)
                nc.scalar.activation(hid[:], hid_ps[:].rearrange("p (b j) -> p b j", b=B), ACT.Gelu, bias=bs1[:])\
                    .then_inc(gelu_done, 1)
                act.wait_ge(xg_ready, 1)
                nc.scalar.copy(xg[:, :, 0, 0:G], xg_ps[:]).then_inc(xg_hi_done, 1)

            @block.vector
            def _(dve):
                n = [0]

                def step(ins):
                    n[0] += 1
                    ins.then_inc(v_chain, 1)
                    dve.wait_ge(v_chain, n[0])

                hi = buf["xn_hi"][:].rearrange("p (b s) -> p b s", b=B)[:, :, 0:B].bitcast(F32)
                lo = buf["xn_lo"][:].rearrange("p (b s) -> p b s", b=B)[:, :, 0:B].bitcast(F32)
                nc.vector.tensor_tensor(xs[:], hi, lo, ALU.add).then_inc(xs_done, 1)
                step(nc.vector.memset(score[:, 0, B:CAND], MASKED))
                step(nc.vector.memset(ones[:], 1.0))
                dve.wait_ge(score_ready, 1)
                dve.wait_ge(loaded, 96)
                nc.vector.tensor_scalar(raw[:], score_ps[:], bs2[:], MASKED, ALU.add, ALU.max).then_inc(raw_done, 1)
                dve.wait_ge(masked, 1)
                for r in range(G // 8):
                    m = best[:, 8 * r:8 * r + 8]
                    step(nc.vector.max(m, score[:, r, :]))
                    step(nc.vector.max_index(best_i[:, 8 * r:8 * r + 8], m, score[:, r, :]))
                    if r < G // 8 - 1:
                        step(nc.vector.match_replace(score[:, r + 1, :], m, score[:, r, :], TAKEN))
                step(nc.vector.tensor_copy(best_f[:], best_i[:]))
                nc.vector.tensor_tensor(wide[:], block_b[:], best_f[:].unsqueeze(1).broadcast_to([B, B, G]), ALU.mult)\
                    .then_inc(wide_done, 1)
                dve.wait_ge(idx_ready, 1)
                nc.vector.tensor_scalar(onehot[:], idx_ps[:].rearrange("p (b g) -> p b g", b=B), iota_p[:], None,
                                        ALU.is_equal).then_inc(onehot_done, 1)
                dve.wait_ge(xg_hi_done, 1)
                step(nc.vector.tensor_tensor(xg[:, :, 1, 0:G], xg_ps[:], xg[:, :, 0, 0:G].bitcast(F32), ALU.subtract))
                step(nc.vector.tensor_copy(xg[:, :, :, G:2 * G].bitcast(F32), xg[:, :, :, 0:G].bitcast(F32)))
                step(nc.vector.tensor_copy(xg[:, :, :, 2 * G:4 * G].bitcast(F32), xg[:, :, :, 0:2 * G].bitcast(F32)))


def attention_stage(nc, buf, dram):
    sc = Scope(nc)
    acc, ident = buf["acc"], buf["ident"]
    U = B * HP
    Q, K, V = range(3)
    with sc:
        w_all = sc.sb("w_all", [P, HP, 6, P], F32R)
        w_raw = sc.sb("w_raw", [P, 2, 3, P])
        w_st = [sc.sb(f"w_st{k}", [P, 6, P], F32R) for k in range(2)]
        wo_st = [sc.sb(f"wo_st{k}", [P, P]) for k in range(2)]
        xst = sc.sb("xst", [P, 2, S], F32R)
        xgst = sc.sb("xgst", [P, 2, P], F32R)
        q_t = [sc.sb(f"q_t{k}", [P, S]) for k in range(2)]
        k_blk = [sc.sb(f"k_blk{k}", [P, NW, SC]) for k in range(2)]
        v_sb = [sc.sb(f"v_sb{k}", [P, NW, P]) for k in range(2)]
        gv_blk = [sc.sb(f"gv_blk{k}", [2 * G, P]) for k in range(2)]
        prob = [sc.sb(f"prob{k}", [P, NW, SC]) for k in range(2)]
        expd = sc.sb("expd", [P, NW, SC])
        shifted = sc.sb("shifted", [P, NW, SC])
        top = sc.sb("att_top", [P, NW, 4])
        den = sc.sb("att_den", [P, NW, 4])
        rec = sc.sb("att_rec", [P, NW, 4])
        pt_loc = sc.sb("pt_loc", [P, NW, 2, WIN])
        pt_glob = sc.sb("pt_glob", [2 * G, NW, WIN])
        att = sc.sb("att", [P, S])
        mask = sc.sb("mask", [P, 2 * WIN], F32R)
        mask_raw = sc.sb("mask_raw", [P, 2 * WIN])
        ident_r = sc.sb("ident_r", [P, P], F32R)
        head_mask = sc.sb("head_mask", [P, 2 * G])
        head_mask_t = sc.sb("head_mask_t", [2 * G, P])
        pj = [sc.ps(f"pj{k}", [P, S]) for k in range(2)]
        sc_ps = sc.ps("sc_ps", [P, NW, S])
        turn = sc.ps("turn", [P, S])
        o_ps = sc.ps("o_ps", [P, S])
        const_in, x_in = sc.sem("a_const_in"), sc.sem("a_x_in")
        w_raw_in, w_in, wo_in = ([sc.sem(f"a_{n}{k}") for k in range(2)] for n in ("w_raw_in", "w_in", "wo_in"))
        names = ["mask_done", "w_hi_done", "w_split", "q_ready", "k_ready", "v_ready", "g_ready", "q_kept", "k_kept", "v_kept",
                 "gk_kept", "gv_kept", "scored", "top_done", "shift_done", "exp_done", "den_done", "rec_done",
                 "prob_done", "turned", "turn_kept", "mixed", "att_kept", "wo_ready", "acc_done"]
        s = {n: sc.sem(f"a_{n}") for n in names}

        start(nc, s.values())
        with nc.Block() as block:
            @block.sync
            def _(sp):
                for name, dst in (("mask", mask_raw), ("head_mask", head_mask), ("head_mask_t", head_mask_t)):
                    sp.dma_start(dst[:], dram[name]).then_inc(const_in, 16)
                for hp in range(2):
                    sp.dma_start(w_raw[:, hp], dram["w_qkv"][hp]).then_inc(w_raw_in[hp], 16)
                with sp.Fori(0, HP // 2 - 1) as pair:
                    for k in range(2):
                        sp.wait_ge(s["w_split"], START + 2 * pair + k + 1)
                        sp.dma_start(w_raw[:, k], dram["w_qkv"][2 * pair + k + 2]).then_inc(w_raw_in[k], 16)

            @block.scalar
            def _(act):
                act.wait_ge(const_in, 48)
                nc.scalar.copy(mask[:], mask_raw[:]).then_inc(s["mask_done"], 1)
                nc.scalar.copy(ident_r[:], ident[:]).then_inc(s["mask_done"], 1)

            @block.vector
            def _(dve):
                with dve.Fori(0, HP // 2) as pair:
                    for k in range(2):
                        hp = 2 * pair + k
                        dve.wait_ge(w_raw_in[k], 16 * (pair + 1))
                        nc.vector.tensor_copy(w_all[:, hp, 0:3, :], w_raw[:, k]).then_inc(s["w_hi_done"], 1)
                        dve.wait_ge(s["w_hi_done"], START + hp + 1)
                        nc.vector.tensor_tensor(w_all[:, hp, 3:6, :], w_raw[:, k],
                                                w_all[:, hp, 0:3, :].bitcast(F32), ALU.subtract)\
                            .then_inc(s["w_split"], 1)

            @block.gpsimd
            def _(pool):
                for k in range(2):
                    nc.gpsimd.memset(k_blk[k][:], 0.0)
                nc.gpsimd.memset(acc[:], 0.0)

        def at_least(eng, sem, count):
            if not isinstance(count, int) or count > 0:
                eng.wait_ge(s[sem], START + count)

        def units(eng, project, score, mix):
            project(0, 0)
            score(0, 0)
            project(1, 1)
            with eng.Fori(0, U // 2 - 1) as pair:
                for k in range(2):
                    mix(2 * pair + k, k, True)
            mix(U - 2, 0, False)
            mix(U - 1, 1, None)

        with nc.Block() as block:
            @block.sync
            def _(sp):
                def stage_x(b):
                    c = bass.ts(b, S)
                    sp.dma_start(xst[:, 0, :].bitcast(F32), buf["xn_hi"][:, c].bitcast(F32)).then_inc(x_in, 16)
                    sp.dma_start(xst[:, 1, :].bitcast(F32), buf["xn_lo"][:, c].bitcast(F32)).then_inc(x_in, 16)
                    sp.dma_start(xgst[:].bitcast(F32), buf["xg"][:, b].bitcast(F32)).then_inc(x_in, 16)

                def stage_w(hp, k):
                    sp.dma_start(w_st[k][:].bitcast(F32), w_all[:, hp].bitcast(F32)).then_inc(w_in[k], 16)

                def stage_wo(hp, k):
                    sp.dma_start(wo_st[k][:], dram["wo"][hp]).then_inc(wo_in[k], 16)

                stage_x(0)
                stage_w(0, 0)
                stage_w(1, 1)
                stage_wo(0, 0)

                def unit(b, pair, k, hp_before):
                    u = HP * b + 2 * pair + k
                    sp.wait_ge(s["g_ready"], START + u - 1)
                    stage_w(2 * pair + k, k)
                    sp.wait_ge(s["wo_ready"], START + u - 2)
                    stage_wo(hp_before, 1 - k)

                def rest_of_batch(b):
                    with sp.Fori(1, HP // 2) as pair:
                        unit(b, pair, 0, 2 * pair - 1)
                        unit(b, pair, 1, 2 * pair)

                rest_of_batch(0)
                with sp.Fori(1, B) as b:
                    sp.wait_ge(s["g_ready"], START + HP * b)
                    stage_x(b)
                    unit(b, 0, 0, HP - 1)
                    unit(b, 0, 1, 0)
                    rest_of_batch(b)
                sp.wait_ge(s["wo_ready"], START + U - 2)
                stage_wo(HP - 1, 1)

            @block.tensor
            def _(pe):
                def three(out, a_hi, a_lo, b_hi, b_lo):
                    nc.tensor.matmul(out, a_hi, b_hi, start=True, stop=False)
                    nc.tensor.matmul(out, a_hi, b_lo, start=False, stop=False)
                    return nc.tensor.matmul(out, a_lo, b_hi, start=False, stop=True)

                def project_q(u, k):
                    pe.wait_ge(w_in[k], 16 * (u // 2 + 1))
                    pe.wait_ge(x_in, 48 * (u // HP + 1))
                    at_least(pe, "v_kept", u)
                    three(pj[0][:], w_st[k][:, Q], w_st[k][:, 3 + Q], xst[:, 0], xst[:, 1]).then_inc(s["q_ready"], 1)

                def project_k(u, k):
                    at_least(pe, "gv_kept", u)
                    three(pj[1][:], w_st[k][:, K], w_st[k][:, 3 + K], xst[:, 0], xst[:, 1]).then_inc(s["k_ready"], 1)

                def project_v(u, k):
                    pe.wait_ge(s["q_kept"], START + u + 1)
                    for w in range(NW):
                        c = slice(w * WIN, (w + 1) * WIN)
                        last = three(pj[0][:, c], xst[:, 0, c], xst[:, 1, c], w_st[k][:, V], w_st[k][:, 3 + V])
                    last.then_inc(s["v_ready"], 1)

                def project_g(u, k):
                    pe.wait_ge(s["k_kept"], START + 2 * u + 2)
                    three(pj[1][:, 0:2 * G], w_st[k][:, K], w_st[k][:, 3 + K],
                          xgst[:, 0, 0:2 * G], xgst[:, 1, 0:2 * G])
                    three(pj[1][:, P:2 * P], xgst[:, 0], xgst[:, 1], w_st[k][:, V], w_st[k][:, 3 + V])\
                        .then_inc(s["g_ready"], 1)

                def project(u, k):
                    project_q(u, k)
                    project_k(u, k)
                    project_v(u, k)
                    project_g(u, k)

                def score(u, k):
                    pe.wait_ge(s["q_kept"], START + u + 1)
                    pe.wait_ge(s["k_kept"], START + 2 * u + 2)
                    pe.wait_ge(s["gk_kept"], START + u + 1)
                    for w in range(NW):
                        if w % 2 == 0:
                            at_least(pe, "shift_done", 4 * u - 2 + w)
                        nc.tensor.matmul(sc_ps[:, w, 0:SC], q_t[k][:, w * WIN:(w + 1) * WIN], k_blk[k][:, w, :],
                                         start=True, stop=False, skip_group_check=True)
                        last = nc.tensor.matmul(sc_ps[:, w, 0:2 * WIN], ident_r[:], mask[:],
                                                start=False, stop=True, skip_group_check=True)
                        if w % 2 == 1:
                            last.then_inc(s["scored"], 1)

                def turn_local(u, k, half):
                    pe.wait_ge(s["prob_done"], START + 4 * u + 2 * half + 2)
                    if half == 0:
                        at_least(pe, "acc_done", u)
                    else:
                        pe.wait_ge(s["turn_kept"], START + 3 * u + 1)
                    for i in range(4):
                        w, h = 2 * half + i // 2, i % 2
                        last = nc.tensor.transpose(turn[:, i * WIN:(i + 1) * WIN],
                                                   prob[k][:, w, h * WIN:(h + 1) * WIN], ident[:])
                    last.then_inc(s["turned"], 1)

                def turn_global(u, k):
                    pe.wait_ge(s["turn_kept"], START + 3 * u + 2)
                    hold(pe, buf)
                    for w in range(NW):
                        last = nc.tensor.transpose(turn[0:2 * G, w * WIN:(w + 1) * WIN], prob[k][:, w, 2 * WIN:SC],
                                                   ident[:])
                    last.then_inc(s["turned"], 1)

                def mix_values(u, k):
                    pe.wait_ge(s["turn_kept"], START + 3 * u + 3)
                    at_least(pe, "att_kept", u)
                    for w in range(NW):
                        o_w = o_ps[:, w * WIN:(w + 1) * WIN]
                        nc.tensor.matmul(o_w, gv_blk[k][:], pt_glob[:, w, :], start=True, stop=False,
                                         skip_group_check=True)
                        for h in range(2):
                            hd = slice(h * HD, (h + 1) * HD)
                            last = nc.tensor.matmul(o_w[hd], v_sb[k][:, w, hd], pt_loc[:, w, h, :],
                                                    start=False, stop=True, skip_group_check=True)
                    last.then_inc(s["mixed"], 1)

                def project_out(u, k):
                    pe.wait_ge(wo_in[k], 16 * (u // 2 + 1))
                    pe.wait_ge(s["att_kept"], START + u + 1)
                    nc.tensor.matmul(turn[:], wo_st[k][:], att[:], start=True, stop=True).then_inc(s["wo_ready"], 1)

                def mix(u, k, ahead):
                    if ahead is not None:
                        score(u + 1, 1 - k)
                    turn_local(u, k, 0)
                    if ahead:
                        project_q(u + 2, k)
                    turn_local(u, k, 1)
                    if ahead:
                        project_k(u + 2, k)
                    turn_global(u, k)
                    if ahead:
                        project_v(u + 2, k)
                    mix_values(u, k)
                    if ahead:
                        project_g(u + 2, k)
                    project_out(u, k)

                pe.wait_ge(s["mask_done"], START + 2)
                units(pe, project, score, mix)

            @block.scalar
            def _(act):
                def keep_q(u, k):
                    act.wait_ge(s["q_ready"], START + u + 1)
                    at_least(act, "scored", 2 * u - 2)
                    nc.scalar.copy(q_t[k][:], pj[0][:]).then_inc(s["q_kept"], 1)

                def keep_k(u, k):
                    act.wait_ge(s["k_ready"], START + u + 1)
                    for h in range(2):
                        hd = slice(h * HD, (h + 1) * HD)
                        nc.scalar.copy(k_blk[k][hd, :, h * WIN:(h + 1) * WIN],
                                       pj[1][hd].rearrange("p (w c) -> p w c", w=NW)).then_inc(s["k_kept"], 1)

                def keep_v(u, k):
                    act.wait_ge(s["v_ready"], START + u + 1)
                    at_least(act, "mixed", u - 1)
                    nc.scalar.copy(v_sb[k][:], pj[0][:].rearrange("p (w c) -> p w c", w=NW)).then_inc(s["v_kept"], 1)

                def exp(u, half):
                    w = slice(2 * half, 2 * half + 2)
                    act.wait_ge(s["shift_done"], START + 4 * u + 2 * half + 2)
                    at_least(act, "prob_done", 4 * u)
                    nc.scalar.activation(expd[:, w, :], shifted[:, w, :], ACT.Exp, scale=SCALE)\
                        .then_inc(s["exp_done"], 1)

                def keep_turned(u, i):
                    act.wait_ge(s["turned"], START + 3 * u + i + 1)
                    if i == 0:
                        at_least(act, "mixed", u)
                    if i < 2:
                        src, dst = turn[:].rearrange("p (w h q) -> p w h q", w=2, h=2), pt_loc[:, 2 * i:2 * i + 2]
                    else:
                        src, dst = turn[0:2 * G].rearrange("p (w q) -> p w q", w=NW), pt_glob[:]
                    nc.scalar.copy(dst, src).then_inc(s["turn_kept"], 1)

                def project(u, k):
                    keep_q(u, k)
                    keep_k(u, k)
                    keep_v(u, k)

                def score(u, k):
                    exp(u, 0)
                    exp(u, 1)

                def mix(u, k, ahead):
                    if ahead is not None:
                        exp(u + 1, 0)
                    keep_turned(u, 0)
                    if ahead:
                        keep_q(u + 2, k)
                    if ahead is not None:
                        exp(u + 1, 1)
                    keep_turned(u, 1)
                    if ahead:
                        keep_k(u + 2, k)
                    keep_turned(u, 2)
                    if ahead:
                        keep_v(u + 2, k)

                units(act, project, score, mix)

            @block.vector
            def _(dve):
                def parts(half):
                    w = slice(2 * half, 2 * half + 2)
                    for c0, c1, t0 in ((0, 2 * WIN, 0), (2 * WIN, SC, 2)):
                        yield (lambda x: x[:, w, c0:c1].rearrange("p w (h c) -> p w h c", h=2),
                               lambda x: x[:, w, t0:t0 + 2], (c1 - c0) // 2)

                def shift(u, half):
                    dve.wait_ge(s["scored"], START + 2 * u + half + 1)
                    at_least(dve, "shift_done", 4 * u + 2 * half - 2)
                    for cols, stat, n in parts(half):
                        nc.vector.tensor_reduce(stat(top), cols(sc_ps), AX.X, ALU.max).then_inc(s["top_done"], 1)
                    dve.wait_ge(s["top_done"], START + 4 * u + 2 * half + 2)
                    for cols, stat, n in parts(half):
                        nc.vector.tensor_tensor(cols(shifted), cols(sc_ps),
                                                stat(top).unsqueeze(3).broadcast_to([P, 2, 2, n]), ALU.subtract)\
                            .then_inc(s["shift_done"], 1)

                def sums(u, half):
                    dve.wait_ge(s["exp_done"], START + 2 * u + half + 1)
                    at_least(dve, "rec_done", 2 * u + half - 1)
                    for cols, stat, n in parts(half):
                        nc.vector.tensor_reduce(stat(den), cols(expd), AX.X, ALU.add).then_inc(s["den_done"], 1)
                    dve.wait_ge(s["den_done"], START + 4 * u + 2 * half + 2)
                    w = slice(2 * half, 2 * half + 2)
                    nc.vector.reciprocal(rec[:, w, :], den[:, w, :]).then_inc(s["rec_done"], 1)

                def keep_g(u, k):
                    dve.wait_ge(s["g_ready"], START + u + 1)
                    at_least(dve, "scored", 2 * u - 2)
                    at_least(dve, "mixed", u - 1)
                    nc.vector.tensor_tensor(k_blk[k][:, :, 2 * WIN:SC],
                                            pj[1][:, 0:2 * G].unsqueeze(1).broadcast_to([P, NW, 2 * G]),
                                            head_mask[:].unsqueeze(1).broadcast_to([P, NW, 2 * G]), ALU.mult)\
                        .then_inc(s["gk_kept"], 1)
                    nc.vector.tensor_tensor(gv_blk[k][:], pj[1][0:2 * G, P:2 * P], head_mask_t[:], ALU.mult)\
                        .then_inc(s["gv_kept"], 1)

                def keep_att(u):
                    dve.wait_ge(s["mixed"], START + u + 1)
                    at_least(dve, "wo_ready", u)
                    nc.vector.tensor_copy(att[:], o_ps[:]).then_inc(s["att_kept"], 1)

                def add_out(u):
                    dve.wait_ge(s["wo_ready"], START + u + 1)
                    at_least(dve, "acc_done", u)
                    b = u // HP
                    nc.vector.tensor_tensor(acc[:, bass.ts(b, S)], turn[:], acc[:, bass.ts(b, S)], ALU.add)\
                        .then_inc(s["acc_done"], 1)

                def softmax(u, k):
                    shift(u, 0)
                    shift(u, 1)
                    at_least(dve, "prob_done", 4 * u)
                    sums(u, 0)
                    sums(u, 1)

                def mix(u, k, ahead):
                    if ahead is not None:
                        softmax(u + 1, 1 - k)
                    keep_att(u)
                    if ahead:
                        keep_g(u + 2, k)
                    add_out(u)

                units(dve, keep_g, softmax, mix)

            @block.gpsimd
            def _(pool):
                def normalise(u, k):
                    for half in range(2):
                        w = slice(2 * half, 2 * half + 2)
                        pool.wait_ge(s["rec_done"], START + 2 * u + half + 1)
                        if half == 0:
                            at_least(pool, "turned", 3 * u - 3)
                        for c0, c1, t0 in ((0, 2 * WIN, 0), (2 * WIN, SC, 2)):
                            cols = lambda x: x[:, w, c0:c1].rearrange("p w (h c) -> p w h c", h=2)
                            nc.gpsimd.tensor_tensor(cols(prob[k]), cols(expd),
                                                    rec[:, w, t0:t0 + 2].unsqueeze(3)
                                                    .broadcast_to([P, 2, 2, (c1 - c0) // 2]), ALU.mult)\
                                .then_inc(s["prob_done"], 1)

                def mix(u, k, ahead):
                    if ahead is not None:
                        normalise(u + 1, 1 - k)

                units(pool, lambda u, k: None, normalise, mix)


def macaron(nc, dram):
    with ExitStack() as keep:
        def sb(name, shape, dt=F32, stack=keep):
            return stack.enter_context(nc.sbuf_tensor(name, shape, dt))

        buf = {
            "X": sb("X", [P, NT, D]),
            "acc": None,
            "logits": sb("logits", [P, NT, E]),
            "weight": sb("weight", [P, NT, 2]),
            "row_in": sb("row_in", [P, SLOT_TILES], U32),
            "slot": sb("slot", [P, NT, 2], U32),
            "owner": sb("owner", [1, SLOT_TILES], U32),
            "ident": sb("ident", [P, P]),
            "gate": sb("gate", [D, E]),
            "iota8": sb("iota8", [P, NT, E]),
        }
        dram["xn"] = nc.dram_tensor("xn_rows", [T, D], F32).ap()
        dram["y"] = nc.dram_tensor("y_rows", [SLOT_TILES * P, D], F32).ap()
        load_constants(nc, keep, buf, dram)

        def experts(tag):
            with ExitStack() as weights:
                buf["w_hi"] = sb(f"w_hi{tag}", [P, E * WC], F32R, weights)
                buf["w_lo"] = sb(f"w_lo{tag}", [P, E * WC], F32R, weights)
                route_stage(nc, buf, dram, f"_r{tag}")
                ffn_stage(nc, buf, dram, f"_f{tag}")

        norm_stage(nc, buf, dram, "_n0", None, "route")
        experts(0)
        with ExitStack() as attention:
            buf["xn_hi"] = sb("xn_hi", [D, T], F32R, attention)
            buf["xn_lo"] = sb("xn_lo", [D, T], F32R, attention)
            buf["acc"] = sb("acc", [D, T], F32, attention)
            buf["xn_head"] = sb("xn_head", [CAND, B, D], F32, attention)
            buf["xg"] = sb("xg", [D, B, 2, P], F32R, attention)
            norm_stage(nc, buf, dram, "_n1", "pairs", "attend")
            select_stage(nc, buf, dram)
            attention_stage(nc, buf, dram)
            norm_stage(nc, buf, dram, "_n2", "acc", "route")
        experts(1)
        norm_stage(nc, buf, dram, "_n3", "pairs", "store")


def kernel(**inputs):
    import concourse.bacc as bacc
    from concourse.bass_utils import run_bass_kernel_spmd

    a = {n.removeprefix("L0_"): np.asarray(v) for n, v in inputs.items()}
    by_pair = lambda w: w.reshape(D, HP, P)
    w_up = a["ffn_wg"].transpose(0, 2, 1), a["ffn_wu"].transpose(0, 2, 1)
    w_down = a["ffn_wd"].transpose(0, 2, 1).reshape(E, J, P, D).transpose(0, 2, 1, 3).reshape(E, P, I)
    key, query = np.arange(WIN)[None, :], np.arange(WIN)[:, None]
    causal = np.where(key > query, np.float32(-3e38), np.float32(0)).astype(np.float32)
    arrays = {
        "x": a["attn_x"].reshape(T, D),
        "gate": a["ffn_gate_w"].T,
        "w_ffn": np.concatenate([*w_up, w_down], axis=2),
        "w_qkv": np.stack([by_pair(a["attn_wq"]), by_pair(a["attn_wk"]), by_pair(a["attn_wv"])]).transpose(2, 1, 0, 3),
        "wo": a["attn_wo"].reshape(HP, P, D),
        "ws1": a["attn_ws1"], "bs1": a["attn_bs1"], "ws2": a["attn_ws2"], "bs2": a["attn_bs2"],
        "ident": np.eye(P, dtype=np.float32),
        "iota8": np.broadcast_to(np.arange(E, dtype=np.float32), (P, NT, E)),
        "lower": np.triu(np.ones((P, P), np.float32), 1),
        "ones": np.ones((P, P), np.float32),
        "iota_row": np.broadcast_to(np.arange(P, dtype=np.float32), (P, P)),
        "token": np.arange(T, dtype=np.float32).reshape(NT, P).T,
        "iota_tile": np.broadcast_to(np.arange(SLOT_TILES, dtype=np.float32)[None, :, None], (1, SLOT_TILES, E)),
        "iota_p": np.arange(CAND, dtype=np.float32)[:, None],
        "block_b": np.repeat(np.eye(B, dtype=np.float32)[:, :, None], G, axis=2),
        "mask": np.concatenate([causal, causal], axis=1),
        "head_mask": np.repeat(np.repeat(np.eye(2, dtype=np.float32), HD, axis=0), G, axis=1),
        "head_mask_t": np.repeat(np.repeat(np.eye(2, dtype=np.float32), G, axis=0), HD, axis=1),
    }
    arrays = {n: np.ascontiguousarray(v) for n, v in arrays.items()}
    nc = bacc.Bacc("TRN2", target_bir_lowering=False, num_devices=1)
    dram = {n: nc.dram_tensor(f"in_{n}", v.shape, mybir.dt.from_np(v.dtype), kind="ExternalInput").ap()
            for n, v in arrays.items()}
    dram["out"] = nc.dram_tensor("out_x", [T, D], F32, kind="ExternalOutput").ap()
    macaron(nc, dram)
    r = run_bass_kernel_spmd(nc, [{f"in_{n}": v for n, v in arrays.items()}], core_ids=[0])
    return r.results[0]["out_x"].reshape(B, S, D)
```

```python
import numpy as np
import concourse.bass as bass
from concourse import mybir
from concourse.alu_op_type import AluOpType as ALU
from contextlib import ExitStack

F32 = mybir.dt.float32
F32R = mybir.dt.float32r
U32 = mybir.dt.uint32
ACT = mybir.ActivationFunctionType
AX = mybir.AxisListType

B, S, D = 8, 512, 128
T = B * S
P = 128
NT = T // P
CH = T // S
TPC = S // P
E, I = 8, 512
J = I // P
H, HD = 16, 64
HP = H * HD // P
GH = 4
WIN = 128
NW = S // WIN
G = 32
SH = D // 4
CAND = B + G
SC = 2 * WIN + 2 * G
KC = NW * (WIN + G)
SLOT_TILES = 2 * T // P + E - 1
WE = 2 * I
EPS = 1e-5
SCALE = 1.0 / HD ** 0.5
TAKEN = float(np.finfo(np.float32).min)
MASKED = float(np.nextafter(np.float32(TAKEN), np.float32(0)))


def hold(eng, buf):
    eng.sem_inc(buf["held"], 1)


START = 1


def start(nc, sems):
    sems = list(sems)
    with nc.Block() as block:
        @block.sync
        def _(sp):
            for sem in sems[0::2]:
                sp.sem_inc(sem, START)

        @block.gpsimd
        def _(pool):
            for sem in sems[1::2]:
                pool.sem_inc(sem, START)


class Step:

    def __init__(self, base, offset=0):
        self.base, self.offset = base, offset

    def after(self, n):
        return Step(self.base, self.offset + n)

    def count(self, per_step, more=0):
        return per_step * self.base + (per_step * self.offset + more + START)

    def wait(self, eng, sem, per_step, more=0):
        count = self.count(per_step, more)
        if not isinstance(count, int) or count > START:
            eng.wait_ge(sem, count)


class Scope:

    def __init__(self, nc):
        self.nc, self.stack, self.own = nc, ExitStack(), []

    def __enter__(self):
        return self

    def __exit__(self, *error):
        if error[0]:
            return
        numbers = sorted(sem.num for sem in self.own)
        firsts = [n for n in numbers if n - 1 not in numbers]
        lasts = [n for n in numbers if n + 1 not in numbers]
        with self.nc.Block() as block:
            @block.gpsimd
            def _(pool):
                for first, last in zip(firsts, lasts):
                    pool.sem_clear(range(first, last + 1))
        self.stack.close()

    def sb(self, name, shape, dt=F32):
        return self.stack.enter_context(self.nc.sbuf_tensor(name, shape, dt))

    def ps(self, name, shape, dt=F32):
        return self.stack.enter_context(self.nc.psum_tensor(name, shape, dt))

    def sem(self, name):
        self.own.append(self.stack.enter_context(self.nc.semaphore(name)))
        return self.own[-1]


def first_stage(nc, sems, buf, dram):
    sc = Scope(nc)
    N = 4
    buf["held"] = sems.enter_context(nc.semaphore("held"))
    with sc:
        w_t = {n: sc.sb(f"{n}_t", [HD, H, D]) for n in ("wq", "wk", "wv", "wo")}
        bank = [sc.ps(f"fold_bank{n}", [P, N, D]) for n in range(8)]
        qk_in, vo_in, loaded, made, hi_done, lo_done = (
            sc.sem(f"fold_{n}") for n in ("qk_in", "vo_in", "loaded", "made", "hi_done", "lo_done"))
        folds = [("qk", "wq", "wk", n) for n in range(0, H, N)] + [("vo", "wv", "wo", n) for n in range(0, H, N)]
        with nc.Block() as block:
            @block.sync
            def _(sp):
                for n, w in w_t.items():
                    sp.dma_start(w[:], dram[f"{n}_t"]).then_inc(qk_in if n in ("wq", "wk") else vo_in, 16)
                sp.dma_start(buf["X"][:], dram["x"].rearrange("(t p) d -> p t d", p=P)).then_inc(loaded, 16)
                for name in ("ident", "gate", "iota8"):
                    sp.dma_start(buf[name][:], dram[name]).then_inc(loaded, 16)
                sp.wait_ge(loaded, 64)

            @block.tensor
            def _(pe):
                for i, (name, a, b, first) in enumerate(folds):
                    pe.wait_ge(qk_in if name == "qk" else vo_in, 32)
                    for n in range(N):
                        last = nc.tensor.matmul(bank[i][:, n, :], w_t[a][:, first + n, :], w_t[b][:, first + n, :],
                                                start=True, stop=True)
                    last.then_inc(made, 1)

            @block.scalar
            def _(act):
                for i, (name, _, _, n) in enumerate(folds):
                    act.wait_ge(made, i + 1)
                    nc.scalar.copy(buf[f"{name}_hi"][:, n:n + N, :], bank[i][:]).then_inc(hi_done, 1)

            @block.vector
            def _(dve):
                for i, (name, _, _, n) in enumerate(folds):
                    dve.wait_ge(hi_done, i + 1)
                    nc.vector.tensor_tensor(buf[f"{name}_lo"][:, n:n + N, :], bank[i][:],
                                            buf[f"{name}_hi"][:, n:n + N, :].bitcast(F32), ALU.subtract)\
                        .then_inc(lo_done, 1)


def norm_stage(nc, buf, dram, tag, source, use):
    sc = Scope(nc)
    X, ident = buf["X"], buf["ident"]
    UPDATES = TPC if source == "pairs" else 1
    norm, route, attend = use != "store", use == "route", use == "attend"
    with sc:
        x_norm = [sc.sb(f"x_norm{k}{tag}", [P, TPC, D]) for k in range(2)]
        stats = [sc.sb(f"stats{k}{tag}", [P, TPC, 6]) for k in range(2)]
        mean_var = [sc.sb(f"mean_var{k}{tag}", [P, TPC, 2]) for k in range(2)]
        std = [sc.sb(f"std{k}{tag}", [P, TPC]) for k in range(2)]
        rstd = [sc.sb(f"rstd{k}{tag}", [P, TPC]) for k in range(2)]
        xnt = [sc.sb(f"xnt{k}{tag}", [P, S]) for k in range(2)]
        eps = sc.sb(f"eps{tag}", [P, 1])
        xnt_ps = [sc.ps(f"xnt_ps{k}{tag}", [P, S]) for k in range(2)]
        lg_ps = [sc.ps(f"lg_ps{k}{tag}", [P, TPC, E]) for k in range(2)]
        if route:
            w_stage = [sc.sb(f"w_stage{k}{tag}", [P, 3 * I]) for k in range(2)]
            w_in = [sc.sem(f"w_in{k}{tag}") for k in range(2)]
        names = (["half_added", "x_updated"] * bool(source)
                 + ["eps_set", "stats_done", "aggr_done", "std_done", "rstd_done", "normed", "turned"] * norm
                 + ["w_hi_done", "w_lo_done", "down_lo_done", "xnt_done", "logits_done", "logits_kept"] * route
                 + ["hi_done", "lo_done", "head_kept"] * attend)
        s = {n: sc.sem(f"{n}{tag}") for n in names}
        stored = [sc.sem(f"stored{k}{tag}") for k in range(2)]
        if source:
            pair_of = [sc.sb(f"pair_of{k}{tag}", [P, TPC, 2, D]) for k in range(2)]
            pairs_in = [sc.sem(f"pairs_in{k}{tag}") for k in range(2)]

        def chunks(eng, first, second, third, late=False):
            def step(c, k, start=False, end=False):
                steps = [(third, c.after(-1), 1 - k)] * (not start) + [(second, c, k)]
                if late:
                    steps.reverse()
                ahead = [(first, c.after(1), 1 - k)] * (not end)
                for do, of, parity in steps + ahead if source else ahead + steps:
                    do(of, parity)

            first(Step(0), 0)
            step(Step(0), 0, start=True)
            with eng.Fori(0, CH - 3, 2) as c:
                for k in range(2):
                    step(Step(c, k + 1), 1 - k)
            step(Step(CH - 1), 1, end=True)
            third(Step(CH - 1), 1)

        def nothing(c, k):
            pass

        def token_rows(name):
            return dram[name].rearrange("(c t p) d -> c p t d", p=P, t=TPC)

        def weights(e):
            down = buf["w_down"][:, bass.ts(e, WE)].rearrange("p (j a d) -> p j a d", j=J, a=2)
            return bass.ts(e, WE), down[:, :, 0, :], down[:, :, 1, :]

        def stage_down(k):
            return w_stage[k][:, WE:].rearrange("p (j d) -> p j d", j=J)

        def index(c):
            return c.base + c.offset

        start(nc, [*s.values(), *stored])
        with nc.Block() as block:
            @block.sync
            def _(sp):
                if route:
                    for k in range(2):
                        sp.dma_start(w_stage[k][:], dram["w_ffn"][k]).then_inc(w_in[k], 16)
                    with sp.Fori(0, E - 3, 2) as e:
                        for k in range(2):
                            sp.wait_ge(s["w_lo_done"], Step(e, k).count(1, 1))
                            sp.wait_ge(s["down_lo_done"], Step(e, k).count(1, 1))
                            sp.dma_start(w_stage[k][:], dram["w_ffn"][e + (k + 2)]).then_inc(w_in[k], 16)

                def store(c, k):
                    if not norm:
                        sp.wait_ge(s["x_updated"], c.count(UPDATES, UPDATES))
                        sp.dma_start(token_rows("out")[index(c)], X[:, bass.ts(index(c), TPC), :])\
                            .then_inc(stored[k], 16)

                chunks(sp, nothing, store, nothing)
                if route or not norm:
                    for k in range(2):
                        sp.wait_ge(stored[k], START + 16 * CH // 2)

            @block.gpsimd
            def _(pool):
                if route:
                    def split_lo(e, k):
                        pool.wait_ge(s["w_hi_done"], e.count(2, 2))
                        up, _, _ = weights(index(e))
                        nc.gpsimd.tensor_tensor(buf["w_lo"][:, up], w_stage[k][:, 0:WE],
                                                buf["w_hi"][:, up].bitcast(F32), ALU.subtract)\
                            .then_inc(s["w_lo_done"], 1)

                    with pool.Fori(0, E - 1, 2) as e:
                        for k in range(2):
                            split_lo(Step(e, k), k)
                if source == "pairs":
                    for c in range(CH):
                        if c >= 2:
                            pool.wait_ge(s["x_updated"], START + UPDATES * (c - 1))
                        for t in range(TPC):
                            for j in range(2):
                                nc.gpsimd.indirect_dma_start(
                                    pair_of[c % 2][:, t, j, :], None, dram["y"],
                                    bass.IndirectOffsetOnAxis(ap=buf["slot"][:, c * TPC + t, j:j + 1], axis=0))\
                                    .then_inc(pairs_in[c % 2], 16)
            @block.tensor
            def _(pe):
                def turn(c, k):
                    if not norm:
                        return
                    pe.wait_ge(s["normed"], c.count(TPC, TPC))
                    c.wait(pe, s["lo_done" if attend else "xnt_done"], 1, -1)
                    for t in range(TPC):
                        last = nc.tensor.transpose(xnt_ps[k][:, t * P:(t + 1) * P], x_norm[k][:, t, :], ident[:])
                    last.then_inc(s["turned"], 1)

                def logits(c, k):
                    if route:
                        pe.wait_ge(s["xnt_done"], c.count(1, 1))
                        c.wait(pe, s["logits_kept"], 1, -1)
                        for t in range(TPC):
                            last = nc.tensor.matmul(lg_ps[k][:, t, :], xnt[k][:, t * P:(t + 1) * P], buf["gate"][:],
                                                    start=True, stop=True)
                        last.then_inc(s["logits_done"], 1)

                chunks(pe, nothing, turn, logits)

            @block.scalar
            def _(act):
                def root(c, k):
                    if norm:
                        act.wait_ge(s["aggr_done"], c.count(TPC, TPC))
                        c.wait(act, s["rstd_done"], 1, -1)
                        nc.scalar.activation(std[k][:], mean_var[k][:, :, 1], ACT.Sqrt, bias=eps[:])\
                            .then_inc(s["std_done"], 1)

                def keep(c, k):
                    if norm:
                        act.wait_ge(s["turned"], c.count(1, 1))
                    if attend:
                        nc.scalar.copy(buf["xn_hi"][:, bass.ts(index(c), S)], xnt_ps[k][:]).then_inc(s["hi_done"], 1)
                        kx_c = buf["kx"][:, bass.ts(index(c), KC)].rearrange("p (w c) -> p w c", w=NW)
                        nc.scalar.copy(kx_c[:, :, 0:WIN], xnt_ps[k][:].rearrange("p (w c) -> p w c", w=NW))\
                            .then_inc(s["hi_done"], 1)
                    if route:
                        act.dma_start(token_rows("xn")[index(c)], x_norm[k][:]).then_inc(stored[k], 16)
                        c.wait(act, s["logits_done"], 1, -1)
                        nc.scalar.copy(xnt[k][:], xnt_ps[k][:]).then_inc(s["xnt_done"], 1)

                if norm:
                    act.wait_ge(s["eps_set"], START + 1)
                def split_hi(e, k):
                    if route:
                        act.wait_ge(w_in[k], 8 * e.base + (8 * (e.offset - k) + 16))
                        up, down_hi, _ = weights(index(e))
                        nc.scalar.copy(buf["w_hi"][:, up], w_stage[k][:, 0:WE]).then_inc(s["w_hi_done"], 1)
                        nc.scalar.copy(down_hi, stage_down(k)).then_inc(s["w_hi_done"], 1)

                chunks(act, root, keep, split_hi)

            @block.vector
            def _(dve):
                def update(c, k):
                    if source == "pairs":
                        dve.wait_ge(pairs_in[k], 128 // 2 * c.base + (128 // 2 * (c.offset - k) + 128))
                        for j in range(2):
                            if j:
                                dve.wait_ge(s["half_added"], c.count(TPC, TPC))
                            for t in range(TPC):
                                at = index(c) * TPC + t
                                nc.vector.scalar_tensor_tensor(
                                    X[:, at, :], pair_of[k][:, t, j, :], buf["weight"][:, at, j:j + 1],
                                    X[:, at, :], ALU.mult, ALU.add).then_inc(s["x_updated" if j else "half_added"], 1)
                    if norm:
                        if source:
                            dve.wait_ge(s["x_updated"], c.count(UPDATES, UPDATES))
                        c.wait(dve, s["normed"], TPC, -TPC)
                        hold(dve, buf)
                        for t in range(TPC):
                            nc.vector.bn_stats(stats[k][:, t, :], X[:, index(c) * TPC + t, :])\
                                .then_inc(s["stats_done"], 1)
                        dve.wait_ge(s["stats_done"], c.count(TPC, TPC))
                        hold(dve, buf)
                        for t in range(TPC):
                            nc.vector.bn_aggr(mean_var[k][:, t, :], stats[k][:, t, :]).then_inc(s["aggr_done"], 1)

                def normalise(c, k):
                    if not norm:
                        return
                    dve.wait_ge(s["std_done"], c.count(1, 1))
                    nc.vector.reciprocal(rstd[k][:], std[k][:]).then_inc(s["rstd_done"], 1)
                    dve.wait_ge(s["rstd_done"], c.count(1, 1))
                    c.wait(dve, s["turned"], 1, -1)
                    if attend:
                        c.wait(dve, s["head_kept"], 1, -1)
                    if route and (not isinstance(c.base, int) or index(c) >= 2):
                        dve.wait_ge(stored[k], 8 * c.base + (8 * (c.offset - k) + START))
                    for t in range(TPC):
                        nc.vector.tensor_scalar(x_norm[k][:, t, :], X[:, index(c) * TPC + t, :],
                                                mean_var[k][:, t, 0:1], rstd[k][:, t:t + 1],
                                                ALU.subtract, ALU.mult).then_inc(s["normed"], 1)
                    if attend:
                        dve.wait_ge(s["normed"], c.count(TPC, 1))
                        nc.vector.tensor_copy(buf["xn_head"][:, index(c), :], x_norm[k][0:CAND, 0, :])\
                            .then_inc(s["head_kept"], 1)

                def keep(c, k):
                    if route:
                        dve.wait_ge(s["w_hi_done"], c.count(2, 2))
                        _, down_hi, down_lo = weights(index(c))
                        nc.vector.tensor_tensor(down_lo, stage_down(k), down_hi.bitcast(F32), ALU.subtract)\
                            .then_inc(s["down_lo_done"], 1)
                    if attend:
                        dve.wait_ge(s["hi_done"], c.count(2, 2))
                        xn = bass.ts(index(c), S)
                        nc.vector.tensor_tensor(buf["xn_lo"][:, xn], xnt_ps[k][:], buf["xn_hi"][:, xn].bitcast(F32),
                                                ALU.subtract).then_inc(s["lo_done"], 1)
                    if route:
                        dve.wait_ge(s["logits_done"], c.count(1, 1))
                        nc.vector.tensor_copy(buf["logits"][:, bass.ts(index(c), TPC), :], lg_ps[k][:])\
                            .then_inc(s["logits_kept"], 1)

                if norm:
                    nc.vector.memset(eps[:], EPS).then_inc(s["eps_set"], 1)
                chunks(dve, update, normalise, keep, late=True)


def route_stage(nc, buf, dram, tag):
    sc = Scope(nc)
    logits = buf["logits"]
    NS = SLOT_TILES
    TN = NS + NS % 2
    with sc:
        top = sc.sb(f"top{tag}", [P, NT, 8])
        top_i = sc.sb(f"top_i{tag}", [P, NT, 8], U32)
        pick = sc.sb(f"pick{tag}", [P, NT, 2])
        diff = sc.sb(f"diff{tag}", [P, NT])
        e2 = sc.sb(f"e2{tag}", [P, NT])
        den = sc.sb(f"den{tag}", [P, NT])
        soft = sc.sb(f"soft{tag}", [P, NT, 2])
        oh = sc.sb(f"oh{tag}", [P, NT, 2, E])
        member = sc.sb(f"member{tag}", [P, NT, E])
        count = [sc.sb(f"count{k}{tag}", [P, NT, E]) for k in range(2)]
        before = sc.sb(f"before{tag}", [P, NT, E])
        padded = sc.sb(f"padded{tag}", [P, E])
        padded_i = sc.sb(f"padded_i{tag}", [P, E], U32)
        tiles_i = sc.sb(f"tiles_i{tag}", [P, E], U32)
        tiles = sc.sb(f"tiles{tag}", [P, E])
        end = [sc.sb(f"end{k}{tag}", [P, E]) for k in range(2)]
        base = sc.sb(f"base{tag}", [P, E])
        where = sc.sb(f"where{tag}", [P, NT, 2, E])
        slot = sc.sb(f"slot{tag}", [P, NT, 2])
        tile_i = sc.sb(f"tile_i{tag}", [P, NT, 2], U32)
        tile_f = sc.sb(f"tile_f{tag}", [P, NT, 2])
        lane = sc.sb(f"lane{tag}", [P, NT, 2])
        past = sc.sb(f"past{tag}", [1, NS, E])
        owner = sc.sb(f"owner{tag}", [1, NS])
        R = 4
        in_lane = [sc.sb(f"in_lane{k}{tag}", [P, R, 2, P], F32R) for k in range(2)]
        in_tile = [sc.sb(f"in_tile{k}{tag}", [P, R, 2, TN], F32R) for k in range(2)]
        rank_ps = sc.ps(f"rank_ps{tag}", [P, NT, E])
        count_ps = sc.ps(f"count_ps{tag}", [P, NT, E])
        table_ps = sc.ps(f"table_ps{tag}", [P, TN])
        names = ["tile_found", "placed", "token_placed", "tabled"]
        s = {n: sc.sem(f"r_{n}{tag}") for n in names}
        consts_in, chain, e2_done, member_done, counted, cleared = (
            sc.sem(f"r_{n}{tag}") for n in ("consts_in", "chain", "e2_done", "member_done", "counted", "cleared"))
        c_lower = sc.sb(f"lower{tag}", [P, P])
        c_ones = sc.sb(f"ones{tag}", [P, P])
        c_iota = sc.sb(f"iota{tag}", [P, P])
        c_token = sc.sb(f"token{tag}", [P, NT])
        c_tile = sc.sb(f"tile_iota{tag}", [1, NS, E])
        zero = sc.sb(f"zero{tag}", [P, P], F32R)
        consts = ((c_lower, "lower"), (c_ones, "ones"), (c_iota, "iota_row"), (c_token, "token"),
                  (c_tile, "iota_tile"))
        start(nc, s.values())
        with nc.Block() as block:
            @block.sync
            def _(sp):
                for dst, name in consts:
                    sp.dma_start(dst[:], dram[name]).then_inc(consts_in, 16)

            @block.scalar
            def _(act):
                act.wait_ge(chain, 2 * NT + 1)
                nc.scalar.activation(e2[:], diff[:], ACT.Exp).then_inc(e2_done, 1)

            @block.gpsimd
            def _(pool):
                pool.wait_ge(consts_in, 16 * len(consts))
                with pool.Fori(0, NT // R - 1, 2) as t:
                    for k in range(2):
                        pool.wait_ge(s["tile_found"], Step(t, k).count(1, 1))
                        nc.gpsimd.tensor_tensor(in_tile[k][:], in_tile[k][:].bitcast(F32),
                                                c_token[:, bass.ds(R * t + R * k, R)].unsqueeze(2).unsqueeze(3)
                                                .broadcast_to([P, R, 2, TN]), ALU.mult).then_inc(s["token_placed"], 1)

            @block.tensor
            def _(pe):
                pe.wait_ge(consts_in, 16 * len(consts))
                pe.wait_ge(member_done, 1)
                nc.tensor.matmul(rank_ps[:], c_lower[:], member[:], start=True, stop=True)
                nc.tensor.matmul(count_ps[:], c_ones[:], member[:], start=True, stop=True).then_inc(counted, 1)
                pe.wait_ge(cleared, 1)
                nc.tensor.matmul(table_ps[:], zero[:], zero[:, 0:TN], start=True, stop=False, skip_group_check=True)\
                    .then_inc(s["tabled"], 2)
                with pe.Fori(0, NT // R - 1, 2) as t:
                    for k in range(2):
                        pe.wait_ge(s["placed"], Step(t, k).count(1, 1))
                        pe.wait_ge(s["token_placed"], Step(t, k).count(1, 1))
                        for q in range(2 * R):
                            last = nc.tensor.matmul(table_ps[:], in_lane[k][:, q // 2, q % 2, :],
                                                    in_tile[k][:, q // 2, q % 2, :], start=False, stop=True,
                                                    skip_group_check=True)
                        last.then_inc(s["tabled"], 1)

            @block.vector
            def _(dve):
                n = [0]

                def step(ins):
                    n[0] += 1
                    ins.then_inc(chain, 1)

                def settled():
                    dve.wait_ge(chain, n[0])

                v = nc.vector
                for t in range(NT):
                    step(v.max(top[:, t, :], logits[:, t, :]))
                settled()
                for t in range(NT):
                    step(v.max_index(top_i[:, t, :], top[:, t, :], logits[:, t, :]))
                step(v.tensor_tensor(diff[:], top[:, :, 1], top[:, :, 0], ALU.subtract))
                settled()
                step(v.tensor_copy(pick[:], top_i[:, :, 0:2]))
                settled()
                for k in range(2):
                    step(v.tensor_tensor(oh[:, :, k, :], buf["iota8"][:],
                                         pick[:, :, k:k + 1].broadcast_to([P, NT, E]), ALU.is_equal))
                v.memset(zero[:].bitcast(F32), 0.0).then_inc(cleared, 1)
                settled()
                v.tensor_tensor(member[:], oh[:, :, 0, :], oh[:, :, 1, :], ALU.add).then_inc(member_done, 1)
                dve.wait_ge(e2_done, 1)
                step(v.tensor_scalar_add(den[:], e2[:], 1.0))
                settled()
                step(v.reciprocal(soft[:, :, 0], den[:]))
                settled()
                step(v.tensor_tensor(soft[:, :, 1], e2[:], soft[:, :, 0], ALU.mult))
                settled()
                step(v.tensor_scalar(buf["weight"][:], soft[:], 0.5, None, ALU.mult))
                dve.wait_ge(counted, 1)
                step(v.tensor_copy(count[0][:], count_ps[:]))
                settled()
                src, d = 0, 1
                while d < NT:
                    step(v.tensor_copy(count[1 - src][:, 0:d, :], count[src][:, 0:d, :]))
                    step(v.tensor_tensor(count[1 - src][:, d:, :], count[src][:, d:, :], count[src][:, :-d, :], ALU.add))
                    settled()
                    src, d = 1 - src, 2 * d
                total = count[src]
                step(v.tensor_tensor(before[:], total[:], count_ps[:], ALU.subtract))
                step(v.tensor_scalar_add(padded[:], total[:, NT - 1, :], float(P - 1)))
                settled()
                step(v.tensor_tensor(before[:], rank_ps[:], before[:], ALU.add))
                step(v.tensor_copy(padded_i[:], padded[:]))
                settled()
                step(v.tensor_scalar(tiles_i[:], padded_i[:], P.bit_length() - 1, None, ALU.logical_shift_right))
                settled()
                step(v.tensor_copy(tiles[:], tiles_i[:]))
                settled()
                step(v.tensor_copy(end[0][:], tiles[:]))
                settled()
                src, d = 0, 1
                while d < E:
                    step(v.tensor_copy(end[1 - src][:, 0:d], end[src][:, 0:d]))
                    step(v.tensor_tensor(end[1 - src][:, d:], end[src][:, d:], end[src][:, :-d], ALU.add))
                    settled()
                    src, d = 1 - src, 2 * d
                ends = end[src]
                step(v.tensor_tensor(base[:], ends[:], tiles[:], ALU.subtract))
                dve.wait_ge(consts_in, 16 * len(consts))
                step(v.tensor_tensor(past[:], c_tile[:], ends[0:1].unsqueeze(1).broadcast_to([1, NS, E]), ALU.is_ge))
                settled()
                step(v.tensor_scalar(base[:], base[:], float(P), None, ALU.mult))
                step(v.tensor_reduce(owner[:], past[:], AX.X, ALU.add))
                settled()
                step(v.tensor_scalar(buf["owner"][:], owner[:], float(E - 1), float(WE), ALU.min, ALU.mult))
                step(v.tensor_tensor(before[:], before[:], base[:].unsqueeze(1).broadcast_to([P, NT, E]), ALU.add))
                settled()
                step(v.tensor_tensor(where[:], oh[:], before[:].unsqueeze(2).broadcast_to([P, NT, 2, E]), ALU.mult))
                settled()
                step(v.tensor_reduce(slot[:], where[:], AX.X, ALU.add))
                settled()
                step(v.tensor_copy(buf["slot"][:], slot[:]))
                settled()
                step(v.tensor_scalar(tile_i[:], buf["slot"][:], P.bit_length() - 1, None, ALU.logical_shift_right))
                settled()
                step(v.tensor_copy(tile_f[:], tile_i[:]))
                settled()
                step(v.scalar_tensor_tensor(lane[:], tile_f[:], float(-P), slot[:], ALU.mult, ALU.add))
                settled()
                at_once = [P, R, 2, TN]
                with dve.Fori(0, NT // R - 1, 2) as t:
                    for k in range(2):
                        dve.wait_ge(s["tabled"], Step(t, k).count(1, 1))
                        tiles_of = bass.ds(R * t + R * k, R)
                        v.tensor_tensor(in_tile[k][:], c_iota[:, 0:TN].unsqueeze(1).unsqueeze(1).broadcast_to(at_once),
                                        tile_f[:, tiles_of, :].unsqueeze(3).broadcast_to(at_once), ALU.is_equal)\
                            .then_inc(s["tile_found"], 1)
                        v.tensor_tensor(in_lane[k][:], c_iota[:].unsqueeze(1).unsqueeze(1).broadcast_to([P, R, 2, P]),
                                        lane[:, tiles_of, :].unsqueeze(3).broadcast_to([P, R, 2, P]), ALU.is_equal)\
                            .then_inc(s["placed"], 1)
                dve.wait_ge(s["tabled"], START + 2 + NT // R)
                step(v.tensor_copy(buf["row_in"][:], table_ps[:, 0:NS]))


def ffn_stage(nc, buf, dram, tag):
    sc = Scope(nc)
    ident, w_hi, w_lo, w_down = buf["ident"], buf["w_hi"], buf["w_lo"], buf["w_down"]
    NS = SLOT_TILES
    M = 4
    with sc:
        x_in = [sc.sb(f"x_in{m}{tag}", [P, D]) for m in range(M)]
        xt_hi = [sc.sb(f"xt_hi{k}{tag}", [D, P], F32R) for k in range(2)]
        xt_lo = [sc.sb(f"xt_lo{k}{tag}", [D, P], F32R) for k in range(2)]
        silu = [sc.sb(f"silu{k}{tag}", [P, I]) for k in range(2)]
        hid = [sc.sb(f"hid{k}{tag}", [P, I]) for k in range(2)]
        ht_hi = [sc.sb(f"ht_hi{k}{tag}", [P, J, P], F32R) for k in range(2)]
        ht_lo = [sc.sb(f"ht_lo{k}{tag}", [P, J, P], F32R) for k in range(2)]
        y_out = [sc.sb(f"y_out{m}{tag}", [P, D]) for m in range(M)]
        gate_ps = [sc.ps(f"gate_ps{k}{tag}", [P, I]) for k in range(2)]
        up_ps = [sc.ps(f"up_ps{k}{tag}", [P, I]) for k in range(2)]
        xt_ps = sc.ps(f"xt_ps{tag}", [D, P])
        ht_ps = sc.ps(f"ht_ps{tag}", [P, J, P])
        y_ps = [sc.ps(f"y_ps{k}{tag}", [P, 2, D]) for k in range(2)]
        gathered = [sc.sem(f"gathered{m}{tag}") for m in range(M)]
        stored = [sc.sem(f"y_stored{m}{tag}") for m in range(M)]
        names = ["x_turned", "x_hi_done", "x_lo_done", "gate_ready", "up_ready", "silu_done", "hid_done", "h_turned",
                 "h_hi_done", "h_lo_done", "y_ready", "y_kept"]
        s = {n: sc.sem(f"f_{n}{tag}") for n in names}

        def tiles(eng, make, turn_h, finish, turn_x):
            turn_x(Step(0), 0)
            turn_x(Step(1), 1)
            make(Step(0), 0)

            def step(i, m, first=False, left=3):
                if left > 1:
                    make(i.after(1), (m + 1) % M)
                if left > 2:
                    turn_x(i.after(2), (m + 2) % M)
                turn_h(i, m)
                if not first:
                    finish(i.after(-1), (m - 1) % M)

            step(Step(0), 0, first=True)
            looped = (NS - 3) // M * M
            with eng.Fori(0, looped - M + 1, M) as i:
                for m in range(1, M + 1):
                    step(Step(i, m), m % M)
            for i in range(looped + 1, NS):
                step(Step(i), i % M, left=min(3, NS - i))
            finish(Step(NS - 1), (NS - 1) % M)

        def nothing(i, m):
            pass

        start(nc, [*s.values(), *stored])
        with nc.Block() as block:
            @block.sync
            def _(sp):
                rows = dram["y"].rearrange("(i p) d -> i p d", p=P)

                def store(i, m):
                    sp.wait_ge(s["y_kept"], i.count(1, 1))
                    sp.dma_start(rows[i.base + i.offset], y_out[m][:]).then_inc(stored[m], 16)

                tiles(sp, nothing, nothing, store, nothing)
                for m in range(M):
                    sp.wait_ge(stored[m], START + 16 * len(range(m, NS, M)))

            @block.gpsimd
            def _(pool):
                for i in range(NS):
                    if i >= M:
                        pool.wait_ge(s["x_turned"], START + i - M + 1)
                    nc.gpsimd.indirect_dma_start(
                        x_in[i % M][:], None, dram["xn"],
                        bass.IndirectOffsetOnAxis(ap=buf["row_in"][:, i:i + 1], axis=0)).then_inc(gathered[i % M], 16)

            @block.tensor
            def _(pe):
                kept = [pe.alloc_register(f"weights{m}{tag}") for m in range(M)]

                def turn_x(i, m):
                    pe.wait_ge(gathered[m], 4 * i.base + (4 * (i.offset - m) + 16))
                    i.wait(pe, s["x_lo_done"], 1)
                    nc.tensor.transpose(xt_ps[:], x_in[m][:], ident[:]).then_inc(s["x_turned"], 1)

                def make(i, m):
                    k = m % 2
                    at = pe.value_load(buf["owner"][0:1, bass.ds(i.base + i.offset, 1)])
                    at = at.with_bounds(min_val=0, max_val=(E - 1) * WE)
                    pe.reg_mov(kept[m], at)
                    pe.wait_ge(s["x_lo_done"], i.count(1, 1))
                    i.wait(pe, s["hid_done"], 1, -1)
                    for n, (out, ready) in enumerate(((gate_ps[k], "gate_ready"), (up_ps[k], "up_ready"))):
                        w = bass.ds(at + n * I, I)
                        nc.tensor.matmul(out[:], xt_hi[k][:], w_hi[:, w], start=True, stop=False)
                        nc.tensor.matmul(out[:], xt_hi[k][:], w_lo[:, w], start=False, stop=False)
                        nc.tensor.matmul(out[:], xt_lo[k][:], w_hi[:, w], start=False, stop=True)\
                            .then_inc(s[ready], 1)

                def turn_h(i, m):
                    pe.wait_ge(s["hid_done"], i.count(1, 1))
                    i.wait(pe, s["h_lo_done"], 1)
                    for j in range(J):
                        last = nc.tensor.transpose(ht_ps[:, j, :], hid[m % 2][:, j * P:(j + 1) * P], ident[:])
                    last.then_inc(s["h_turned"], 1)

                def finish(i, m):
                    k = m % 2
                    at = bass.RuntimeValue.of_register_unchecked(kept[m]).with_bounds(min_val=0, max_val=(E - 1) * WE)
                    pe.wait_ge(s["h_lo_done"], i.count(1, 1))
                    i.wait(pe, s["y_kept"], 1, -1)
                    for j in range(J):
                        w = w_down[:, bass.ds(at + 2 * j * D, 2 * D)]
                        hi = w_down[:, bass.ds(at + 2 * j * D, D)]
                        nc.tensor.matmul(y_ps[k][:], ht_hi[k][:, j, :], w, start=j == 0, stop=False,
                                         skip_group_check=True)
                        last = nc.tensor.matmul(y_ps[k][:, 0, :], ht_lo[k][:, j, :], hi, start=False, stop=j == J - 1,
                                                skip_group_check=True)
                    last.then_inc(s["y_ready"], 1)

                tiles(pe, make, turn_h, finish, turn_x)

            @block.scalar
            def _(act):
                def turn_x(i, m):
                    act.wait_ge(s["x_turned"], i.count(1, 1))
                    i.wait(act, s["up_ready"], 1, -1)
                    nc.scalar.copy(xt_hi[m % 2][:], xt_ps[:]).then_inc(s["x_hi_done"], 1)

                def make(i, m):
                    act.wait_ge(s["gate_ready"], i.count(1, 1))
                    i.wait(act, s["hid_done"], 1, -1)
                    nc.scalar.activation(silu[m % 2][:], gate_ps[m % 2][:], ACT.Silu).then_inc(s["silu_done"], 1)

                def turn_h(i, m):
                    act.wait_ge(s["h_turned"], i.count(1, 1))
                    i.wait(act, s["y_ready"], 1, -1)
                    nc.scalar.copy(ht_hi[m % 2][:], ht_ps[:]).then_inc(s["h_hi_done"], 1)

                tiles(act, make, turn_h, nothing, turn_x)

            @block.vector
            def _(dve):
                def turn_x(i, m):
                    dve.wait_ge(s["x_hi_done"], i.count(1, 1))
                    nc.vector.tensor_tensor(xt_lo[m % 2][:], xt_ps[:], xt_hi[m % 2][:].bitcast(F32), ALU.subtract)\
                        .then_inc(s["x_lo_done"], 1)

                def make(i, m):
                    dve.wait_ge(s["silu_done"], i.count(1, 1))
                    dve.wait_ge(s["up_ready"], i.count(1, 1))
                    i.wait(dve, s["h_turned"], 1, -1)
                    nc.vector.tensor_tensor(hid[m % 2][:], up_ps[m % 2][:], silu[m % 2][:], ALU.mult)\
                        .then_inc(s["hid_done"], 1)

                def turn_h(i, m):
                    dve.wait_ge(s["h_hi_done"], i.count(1, 1))
                    nc.vector.tensor_tensor(ht_lo[m % 2][:], ht_ps[:], ht_hi[m % 2][:].bitcast(F32), ALU.subtract)\
                        .then_inc(s["h_lo_done"], 1)

                def finish(i, m):
                    dve.wait_ge(s["y_ready"], i.count(1, 1))
                    if not isinstance(i.base, int) or i.offset + i.base >= M:
                        dve.wait_ge(stored[m], 4 * i.base + (4 * (i.offset - m) + START))
                    nc.vector.tensor_reduce(y_out[m][:], y_ps[m % 2][:].rearrange("p a d -> p d a"), AX.X, ALU.add)\
                        .then_inc(s["y_kept"], 1)

                tiles(dve, make, turn_h, finish, turn_x)


def select_stage(nc, buf, dram):
    sc = Scope(nc)
    with sc:
        ws1 = sc.sb("ws1", [D, SH])
        bs1 = sc.sb("bs1", [SH, 1])
        ws2 = sc.sb("ws2", [SH, 1])
        bs2 = sc.sb("bs2", [B, 1])
        iota_p = sc.sb("iota_p", [CAND, 1])
        block_b = sc.sb("block_b", [B, B, G])
        hid = sc.sb("sel_hid", [SH, B, B])
        raw = sc.sb("raw", [B, B])
        score = sc.sb("score", [B, 4, CAND])
        best = sc.sb("best", [B, G])
        best_i = sc.sb("best_i", [B, G], U32)
        best_f = sc.sb("best_f", [B, G])
        wide = sc.sb("wide", [B, B, G])
        ones = sc.sb("ones", [B, CAND])
        onehot = sc.sb("onehot", [CAND, B, G])
        hid_ps = sc.ps("sel_hid_ps", [SH, B * B])
        score_ps = sc.ps("score_ps", [B, B])
        idx_ps = sc.ps("idx_ps", [CAND, B * G])
        xg_ps = sc.ps("xg_ps", [D, B, G])
        xg_hi, xg_lo = buf["xg_hi"], buf["xg_lo"]
        kx = buf["kx"][:].rearrange("p (b w c) -> p b w c", b=B, w=NW)
        v_chain, loaded, hid_ready, gelu_done, score_ready, masked, wide_done, idx_ready, onehot_done, \
            xg_ready, xg_hi_done, xg_done = (sc.sem(f"sel_{n}") for n in (
                "v_chain", "loaded", "hid_ready", "gelu_done", "score_ready", "masked", "wide_done",
                "idx_ready", "onehot_done", "xg_ready", "xg_hi_done", "xg_done"))
        raw_done = sc.sem("sel_raw_done")
        with nc.Block() as block:
            @block.sync
            def _(sp):
                sp.dma_start(ws1[:], dram["ws1"]).then_inc(loaded, 16)
                sp.dma_start(bs1[:], dram["bs1"].unsqueeze(1)).then_inc(loaded, 16)
                sp.dma_start(ws2[:], dram["ws2"]).then_inc(loaded, 16)
                sp.dma_start(bs2[:], dram["bs2"].partition_broadcast(B)).then_inc(loaded, 16)
                sp.dma_start(iota_p[:], dram["iota_p"]).then_inc(loaded, 16)
                sp.dma_start(block_b[:], dram["block_b"]).then_inc(loaded, 16)

            @block.gpsimd
            def _(pool):
                pool.wait_ge(raw_done, 1)
                nc.gpsimd.affine_select(out=score[:, 0, 0:B], in_=raw[:], pattern=[[-1, B]], compare_op=ALU.is_ge,
                                        fill=MASKED, base=0, channel_multiplier=1).then_inc(masked, 1)

            @block.tensor
            def _(pe):
                pe.wait_ge(loaded, 96)
                nc.tensor.matmul(hid_ps[:], ws1[:], kx[:, :, 0, 0:B], start=True, stop=True).then_inc(hid_ready, 1)
                pe.wait_ge(gelu_done, 1)
                for j in range(B):
                    last = nc.tensor.matmul(score_ps[:, j:j + 1], hid[:, :, j], ws2[:], start=True, stop=True)
                last.then_inc(score_ready, 1)
                pe.wait_ge(wide_done, 1)
                nc.tensor.matmul(idx_ps[:], ones[:], wide[:], start=True, stop=True).then_inc(idx_ready, 1)
                pe.wait_ge(onehot_done, 1)
                for b in range(B):
                    last = nc.tensor.matmul(xg_ps[:, b, :], buf["xn_head"][:, b, :], onehot[:, b, :],
                                            start=True, stop=True)
                last.then_inc(xg_ready, 1)

            @block.scalar
            def _(act):
                act.wait_ge(hid_ready, 1)
                act.wait_ge(loaded, 96)
                nc.scalar.activation(hid[:], hid_ps[:].rearrange("p (b j) -> p b j", b=B), ACT.Gelu, bias=bs1[:])\
                    .then_inc(gelu_done, 1)
                act.wait_ge(xg_ready, 1)
                nc.scalar.copy(xg_hi[:], xg_ps[:]).then_inc(xg_hi_done, 1)

            @block.vector
            def _(dve):
                n = [0]

                def step(ins):
                    n[0] += 1
                    ins.then_inc(v_chain, 1)
                    dve.wait_ge(v_chain, n[0])

                step(nc.vector.memset(score[:, 0, B:CAND], MASKED))
                step(nc.vector.memset(ones[:], 1.0))
                dve.wait_ge(score_ready, 1)
                dve.wait_ge(loaded, 96)
                nc.vector.tensor_scalar(raw[:], score_ps[:], bs2[:], MASKED, ALU.add, ALU.max).then_inc(raw_done, 1)
                dve.wait_ge(masked, 1)
                for r in range(G // 8):
                    m = best[:, 8 * r:8 * r + 8]
                    step(nc.vector.max(m, score[:, r, :]))
                    step(nc.vector.max_index(best_i[:, 8 * r:8 * r + 8], m, score[:, r, :]))
                    if r < G // 8 - 1:
                        step(nc.vector.match_replace(score[:, r + 1, :], m, score[:, r, :], TAKEN))
                step(nc.vector.tensor_copy(best_f[:], best_i[:]))
                nc.vector.tensor_tensor(wide[:], block_b[:], best_f[:].unsqueeze(1).broadcast_to([B, B, G]), ALU.mult)\
                    .then_inc(wide_done, 1)
                dve.wait_ge(idx_ready, 1)
                nc.vector.tensor_scalar(onehot[:], idx_ps[:].rearrange("p (b g) -> p b g", b=B), iota_p[:], None,
                                        ALU.is_equal).then_inc(onehot_done, 1)
                dve.wait_ge(xg_hi_done, 1)
                step(nc.vector.tensor_tensor(xg_lo[:], xg_ps[:], xg_hi[:].bitcast(F32), ALU.subtract))
                step(nc.vector.tensor_copy(kx[:, :, :, WIN:], xg_ps[:].unsqueeze(2).broadcast_to([D, B, NW, G])))


def global_values_stage(nc, buf, dram):
    sc = Scope(nc)
    with sc:
        rows = sc.sb("gvo_by_token", [P, 2, GH, H // GH, D])
        bank = [sc.ps(f"gvo_bank{n}", [P, GH, D]) for n in range(8)]
        made, kept, written = (sc.sem(f"gvo_{n}") for n in ("made", "kept", "written"))
        jobs = [(half, n) for half in range(2) for n in range(0, H, GH)]
        with nc.Block() as block:
            @block.sync
            def _(sp):
                by_token = dram["gvo"].rearrange("(h g) b n d -> b g h (n d)", g=G)
                for b in range(B):
                    half, at = b // (B // 2), b % (B // 2) * G
                    sp.wait_ge(kept, H // GH * (half + 1))
                    sp.dma_start(by_token[b], rows[at:at + G, half].rearrange("p h n d -> p h (n d)"))\
                        .then_inc(written, 16)
                sp.wait_ge(written, 16 * B)

            @block.tensor
            def _(pe):
                for i, (half, n) in enumerate(jobs):
                    hi, lo = (buf[x][:, bass.ts(half, B // 2), :] for x in ("xg_hi", "xg_lo"))
                    nc.tensor.matmul(bank[i][:], hi, buf["vo_hi"][:, n:n + GH, :], start=True, stop=False)
                    nc.tensor.matmul(bank[i][:], hi, buf["vo_lo"][:, n:n + GH, :], start=False, stop=False)
                    nc.tensor.matmul(bank[i][:], lo, buf["vo_hi"][:, n:n + GH, :], start=False, stop=True)\
                        .then_inc(made, 1)

            @block.scalar
            def _(act):
                for i, (half, n) in enumerate(jobs):
                    act.wait_ge(made, i + 1)
                    nc.scalar.copy(rows[:, half, :, n // GH, :], bank[i][:]).then_inc(kept, 1)


def attention_stage(nc, buf, dram):
    sc = Scope(nc)
    X, ident, kx = buf["X"], buf["ident"], buf["kx"]
    gvo = buf["gvo"][:].rearrange("p n d -> p (n d)")
    with sc:
        xst = sc.sb("xst", [D, 2, NW, WIN], F32R)
        q_t = [sc.sb(f"q_t{k}", [D, 2, S]) for k in range(2)]
        vo = [sc.sb(f"vo{k}", [P, NW, GH, D]) for k in range(2)]
        prob = [sc.sb(f"prob{k}", [P, NW, 2, WIN]) for k in range(2)]
        prob_glob = [sc.sb(f"prob_glob{k}", [P, NW, GH, G]) for k in range(2)]
        expd = [sc.sb(f"expd{k}", [P, NW, SC]) for k in range(2)]
        top = sc.sb("att_top", [P, NW, 4])
        den = sc.sb("att_den", [P, NW, 4])
        rec = sc.sb("att_rec", [P, NW, 4])
        pt_loc = sc.sb("pt_loc", [P, NW, 2, WIN])
        pt_glob = sc.sb("pt_glob", [GH * G, NW, WIN])
        mask = sc.sb("mask", [P, WIN])
        pj = [sc.ps(f"pj{k}", [P, S]) for k in range(2)]
        sc_ps = sc.ps("sc_ps", [P, NW, S])
        turn = sc.ps("turn", [P, S])
        o_ps = sc.ps("o_ps", [P, NW, D])
        gvo_in, const_in, x_in = sc.sem("a_gvo_in"), sc.sem("a_const_in"), [sc.sem(f"a_x_in{h}") for h in range(2)]
        names = ["masked", "q_ready", "q_kept", "vo_ready", "vo_kept", "scored", "top_done", "shift_done",
                 "exp_done", "den_done", "rec_done", "prob_done", "turned", "turn_kept", "g_turned", "g_kept",
                 "mixed", "x_added"]
        s = {n: sc.sem(f"a_{n}") for n in names}

        def units(eng, first_vo, project, score, mix):
            first_vo()
            project(Step(0), 0)
            score(Step(0), 0)
            project(Step(0, 1), 1)
            with eng.Fori(0, (B - 2) * HP + 1, HP) as u:
                for hp in range(HP):
                    mix(Step(u, hp), hp, 2)
            for hp in range(HP):
                mix(Step((B - 1) * HP, hp), hp, min(2, HP - 1 - hp))

        def nothing(*_):
            pass

        def in_batch(u, columns):
            base = u.base * (columns // HP) if columns >= HP else u.base // (HP // columns)
            return base + u.offset // HP * columns

        start(nc, s.values())
        with nc.Block() as block:
            @block.sync
            def _(sp):
                sp.dma_start(mask[:], dram["mask"]).then_inc(const_in, 16)

                def stage_x(u, half):
                    at = in_batch(u, S) + half * S // 2
                    for part, src in enumerate(("xn_hi", "xn_lo")):
                        sp.dma_start(xst[:, part, 2 * half:2 * half + 2, :].bitcast(F32),
                                     buf[src][:, bass.ds(at, S // 2)].bitcast(F32).rearrange("p (w c) -> p w c", w=2))\
                            .then_inc(x_in[half], 16)

                stage_x(Step(0), 0)
                stage_x(Step(0), 1)
                sp.dma_start(gvo, dram["gvo"].rearrange("p b n d -> p (b n d)")).then_inc(gvo_in, 16)
                with sp.Fori(0, (B - 2) * HP + 1, HP) as u:
                    for half in range(2):
                        sp.wait_ge(s["vo_ready"], Step(u, HP - 4 + half).count(2, 2 + NW))
                        stage_x(Step(u, HP), half)

            @block.tensor
            def _(pe):
                def three(out, a_hi, a_lo, b_hi, b_lo, ready, passes):
                    for n in passes:
                        a, b = ((a_hi, b_hi), (a_hi, b_lo), (a_lo, b_hi))[n]
                        last = nc.tensor.matmul(out, a, b, start=n == 0, stop=n == 2)
                    if n == 2:
                        last.then_inc(ready, 1)

                def project_q(u, hp, h, vo_made, passes=range(3)):
                    if 0 in passes:
                        pe.wait_ge(s["vo_kept"], vo_made)
                        u.wait(pe, s["q_kept"], 2, h - 1)
                    x = bass.ds(in_batch(u, S), S)
                    three(pj[h][:], buf["qk_hi"][:, 2 * hp + h, :], buf["qk_lo"][:, 2 * hp + h, :],
                          buf["xn_hi"][:, x], buf["xn_lo"][:, x], s["q_ready"], passes)

                def project_vo(group, w, passes=range(3)):
                    heads = slice(group * GH, (group + 1) * GH)
                    three(pj[w % 2][:], xst[:, 0, w, :], xst[:, 1, w, :], buf["vo_hi"][:, heads, :],
                          buf["vo_lo"][:, heads, :], s["vo_ready"], passes)

                def first_vo():
                    for half in range(2):
                        pe.wait_ge(x_in[half], 32)
                    for w in range(NW):
                        if w >= 2:
                            pe.wait_ge(s["vo_kept"], START + w - 1)
                        project_vo(0, w)

                def project(u, hp):
                    for h in range(2):
                        project_q(u, hp, h, START + NW)

                def score(u, hp):
                    pe.wait_ge(s["q_kept"], u.count(2, 2))
                    for w in range(NW):
                        if w % 2 == 0:
                            u.wait(pe, s["shift_done"], 4, w - 2)
                        keys = bass.ds(in_batch(u, KC) + w * (WIN + G), WIN + G)
                        for h in range(2):
                            last = nc.tensor.matmul(
                                sc_ps[:, w, h * (WIN + G):(h + 1) * (WIN + G)],
                                q_t[hp % 2][:, h, w * WIN:(w + 1) * WIN], kx[:, keys],
                                start=h == 0, stop=True, skip_group_check=True)
                        if w % 2 == 1:
                            last.then_inc(s["scored"], 1)

                def turn_local(u, hp, half):
                    pe.wait_ge(s["prob_done"], u.count(4, 2 * half + 2))
                    if half == 0 and hp % 2 == 0:
                        pe.wait_ge(s["g_kept"], u.count(1, 0))
                    else:
                        pe.wait_ge(s["turn_kept"], u.count(2, half))
                    for i in range(4):
                        w, h = 2 * half + i // 2, i % 2
                        last = nc.tensor.transpose(turn[:, i * WIN:(i + 1) * WIN], prob[hp % 2][:, w, h, :], ident[:])
                    last.then_inc(s["turned"], 1)

                def turn_global(u, hp):
                    if hp % 2 == 1:
                        pe.wait_ge(s["turn_kept"], u.count(2, 2))
                        for w in range(NW):
                            last = nc.tensor.transpose(turn[:, w * WIN:(w + 1) * WIN],
                                                       prob_glob[hp // 2 % 2][:, w, :, :], ident[:])
                        last.then_inc(s["g_turned"], 2)

                def mix_values(u, hp):
                    pe.wait_ge(s["turn_kept"], u.count(2, 2))
                    pe.wait_ge(s["vo_kept"], u.count(2, NW - 2 * (hp % 2)))
                    if hp == 0:
                        pe.wait_ge(s["x_added"], START + u.base // HP)
                    first = hp == 0
                    values = vo[hp // 2 % 2]
                    for w in range(NW):
                        for h in range(2):
                            last = nc.tensor.matmul(o_ps[:, w, :], pt_loc[:, w, h, :],
                                                    values[:, w, 2 * (hp % 2) + h, :],
                                                    start=first and w == 0 and h == 0, stop=True,
                                                    skip_group_check=True)
                    if hp % 2 == 1:
                        if hp == 1:
                            pe.wait_ge(gvo_in, 16)
                        pe.wait_ge(s["g_kept"], u.count(1, 1))
                        group = bass.ds(u.base * (D // 2) + u.offset // 2 * D, D)
                        for w in range(NW):
                            last = nc.tensor.matmul(o_ps[:, w, :], pt_glob[:, w, :], gvo[:, group],
                                                    start=False, stop=True, skip_group_check=True)
                    last.then_inc(s["mixed"], 1)

                def mix(u, hp, ahead):
                    if ahead:
                        score(u.after(1), (hp + 1) % HP)

                    def q(h, *passes):
                        if ahead == 2:
                            project_q(u.after(2), (hp + 2) % HP, h, u.count(2, NW - 1 + h), passes)

                    def v(j, *passes):
                        if ahead == 2:
                            if 0 in passes:
                                pe.wait_ge(s["q_kept"], u.after(2).count(2, j + 1))
                                if j == 0 and hp >= HP - 2:
                                    pe.wait_ge(x_in[hp % 2], 32 // HP * u.base + 64)
                            project_vo((hp // 2 + 1) % (H // GH), 2 * (hp % 2) + j, passes)

                    turn_local(u, hp, 0)
                    q(0, 0, 1, 2)
                    q(1, 0)
                    turn_local(u, hp, 1)
                    q(1, 1, 2)
                    v(0, 0, 1)
                    turn_global(u, hp)
                    v(0, 2)
                    if hp % 2 == 1:
                        v(1, 0, 1, 2)
                        mix_values(u, hp)
                    else:
                        mix_values(u, hp)
                        v(1, 0, 1, 2)

                units(pe, first_vo, project, score, mix)

            @block.scalar
            def _(act):
                def keep_q(u, hp, h):
                    act.wait_ge(s["q_ready"], u.count(2, h + 1))
                    u.wait(act, s["scored"], 2, -2)
                    nc.scalar.copy(q_t[hp % 2][:, h, :], pj[h][:]).then_inc(s["q_kept"], 1)

                def keep_vo(k, w):
                    nc.scalar.copy(vo[k][:, w, :, :], pj[w % 2][:].rearrange("p (h d) -> p h d", h=GH))\
                        .then_inc(s["vo_kept"], 1)

                def first_vo():
                    for w in range(NW):
                        act.wait_ge(s["vo_ready"], START + w + 1)
                        keep_vo(0, w)

                def exp(u, hp, half):
                    w = slice(2 * half, 2 * half + 2)
                    act.wait_ge(s["shift_done"], u.count(4, 2 * half + 2))
                    nc.scalar.activation(expd[hp % 2][:, w, :], expd[hp % 2][:, w, :], ACT.Exp, scale=SCALE)\
                        .then_inc(s["exp_done"], 1)

                def keep_turned(u, half):
                    act.wait_ge(s["turned"], u.count(2, half + 1))
                    if half == 0:
                        act.wait_ge(s["mixed"], u.count(1, 0))
                    nc.scalar.copy(pt_loc[:, 2 * half:2 * half + 2], turn[:].rearrange("p (w h q) -> p w h q", w=2, h=2))\
                        .then_inc(s["turn_kept"], 1)

                def keep_global(u, hp):
                    if hp % 2 == 1:
                        act.wait_ge(s["g_turned"], u.count(1, 1))
                        nc.scalar.copy(pt_glob[:], turn[:].rearrange("p (w q) -> p w q", w=NW))\
                            .then_inc(s["g_kept"], 2)

                def project(u, hp):
                    for h in range(2):
                        keep_q(u, hp, h)

                def score(u, hp):
                    for half in range(2):
                        exp(u, hp, half)

                def mix(u, hp, ahead):
                    for i in range(2):
                        keep_turned(u, i)
                        if ahead == 2:
                            keep_q(u.after(2), hp + 2, i)
                    keep_global(u, hp)
                    if ahead:
                        score(u.after(1), hp + 1)
                    if ahead == 2:
                        for j in range(2):
                            act.wait_ge(s["vo_ready"], u.count(2, NW + j + 1))
                            act.wait_ge(s["mixed"], u.count(1, -(hp % 2)))
                            keep_vo((hp // 2 + 1) % 2, 2 * (hp % 2) + j)

                units(act, first_vo, project, score, mix)

            @block.vector
            def _(dve):
                def parts(half):
                    w = slice(2 * half, 2 * half + 2)
                    for c0, p0, t0, n in ((0, 0, 0, WIN), (2 * WIN, WIN, 2, G)):
                        yield (sc_ps[:, w, 0:SC].rearrange("p w (h c) -> p w h c", h=2)[:, :, :, p0:p0 + n],
                               lambda x, c0=c0, n=n: x[:, w, c0:c0 + 2 * n].rearrange("p w (h c) -> p w h c", h=2),
                               lambda x, t0=t0: x[:, w, t0:t0 + 2], n)

                def shift(u, hp, half):
                    dve.wait_ge(s["scored"], u.count(2, half + 1))
                    if half == 0:
                        u.wait(dve, s["prob_done"], 4, -4)
                    u.wait(dve, s["shift_done"], 4, 2 * half - 2)
                    (scores, cols, stat, n), (g_scores, g_cols, g_stat, g_n) = parts(half)
                    local = cols(expd[hp % 2])
                    nc.vector.tensor_tensor(local, scores, mask[:].unsqueeze(1).unsqueeze(1)
                                            .broadcast_to([P, 2, 2, WIN]), ALU.add).then_inc(s["masked"], 1)
                    nc.vector.tensor_reduce(g_stat(top), g_scores, AX.X, ALU.max).then_inc(s["top_done"], 1)
                    dve.wait_ge(s["masked"], u.count(2, half + 1))
                    nc.vector.tensor_reduce(stat(top), local, AX.X, ALU.max).then_inc(s["top_done"], 1)
                    dve.wait_ge(s["top_done"], u.count(4, 2 * half + 2))
                    for src, dst, top_of, width in ((local, local, stat(top), n),
                                                    (g_scores, g_cols(expd[hp % 2]), g_stat(top), g_n)):
                        nc.vector.tensor_tensor(dst, src, top_of.unsqueeze(3).broadcast_to([P, 2, 2, width]),
                                                ALU.subtract).then_inc(s["shift_done"], 1)

                def sums(u, hp, half):
                    dve.wait_ge(s["exp_done"], u.count(2, half + 1))
                    u.wait(dve, s["rec_done"], 2, half - 1)
                    for scores, cols, stat, n in parts(half):
                        nc.vector.tensor_reduce(stat(den), cols(expd[hp % 2]), AX.X, ALU.add)\
                            .then_inc(s["den_done"], 1)
                    dve.wait_ge(s["den_done"], u.count(4, 2 * half + 2))
                    u.wait(dve, s["prob_done"], 4, 2 * half - 2)
                    w = slice(2 * half, 2 * half + 2)
                    nc.vector.reciprocal(rec[:, w, :], den[:, w, :]).then_inc(s["rec_done"], 1)

                def softmax(u, hp):
                    for step in (shift, sums):
                        for half in range(2):
                            step(u, hp, half)

                def mix(u, hp, ahead):
                    if ahead:
                        softmax(u.after(1), hp + 1)
                    if hp == HP - 1:
                        dve.wait_ge(s["mixed"], u.count(1, 1))
                        x = X[:, bass.ds(in_batch(u, NW), NW), :]
                        nc.vector.tensor_tensor(x, x, o_ps[:], ALU.add).then_inc(s["x_added"], 1)

                dve.wait_ge(const_in, 16)
                units(dve, nothing, nothing, softmax, mix)

            @block.gpsimd
            def _(pool):
                def normalise(u, hp):
                    for half in range(2):
                        pool.wait_ge(s["rec_done"], u.count(2, half + 1))
                        if half == 0:
                            u.wait(pool, s["turned"], 2, -2)
                            if hp % 2 == 0:
                                u.wait(pool, s["g_turned"], 1, -2)
                        w = slice(2 * half, 2 * half + 2)
                        pair = slice(2 * (hp % 2), 2 * (hp % 2) + 2)
                        for dst, c0, n, t0 in ((prob[hp % 2][:, w], 0, WIN, 0),
                                               (prob_glob[hp // 2 % 2][:, w, pair, :], 2 * WIN, G, 2)):
                            nc.gpsimd.tensor_tensor(
                                dst, expd[hp % 2][:, w, c0:c0 + 2 * n].rearrange("p w (h c) -> p w h c", h=2),
                                rec[:, w, t0:t0 + 2].unsqueeze(3).broadcast_to([P, 2, 2, n]), ALU.mult)\
                                .then_inc(s["prob_done"], 1)

                def mix(u, hp, ahead):
                    if ahead:
                        normalise(u.after(1), (hp + 1) % HP)

                units(pool, nothing, nothing, normalise, mix)


def macaron(nc, dram):
    with ExitStack() as keep:
        def sb(name, shape, dt=F32, stack=keep):
            return stack.enter_context(nc.sbuf_tensor(name, shape, dt))

        buf = {
            "X": sb("X", [P, NT, D]),
            "logits": sb("logits", [P, NT, E]),
            "weight": sb("weight", [P, NT, 2]),
            "row_in": sb("row_in", [P, SLOT_TILES], U32),
            "slot": sb("slot", [P, NT, 2], U32),
            "owner": sb("owner", [1, SLOT_TILES], U32),
            "ident": sb("ident", [P, P]),
            "gate": sb("gate", [D, E]),
            "iota8": sb("iota8", [P, NT, E]),
            "qk_hi": sb("qk_hi", [D, H, D], F32R), "qk_lo": sb("qk_lo", [D, H, D], F32R),
            "vo_hi": sb("vo_hi", [D, H, D], F32R), "vo_lo": sb("vo_lo", [D, H, D], F32R),
        }
        dram["xn"] = nc.dram_tensor("xn_rows", [T, D], F32).ap()
        dram["gvo"] = nc.dram_tensor("gvo_rows", [GH * G, B, H // GH, D], F32).ap()
        dram["y"] = nc.dram_tensor("y_rows", [SLOT_TILES * P, D], F32).ap()
        first_stage(nc, keep, buf, dram)

        def experts(tag):
            with ExitStack() as weights:
                for name in ("w_hi", "w_lo", "w_down"):
                    buf[name] = sb(f"{name}{tag}", [P, E * WE], F32R, weights)
                norm_stage(nc, buf, dram, f"_n{tag}", None, "route")
                route_stage(nc, buf, dram, f"_r{tag}")
                ffn_stage(nc, buf, dram, f"_f{tag}")

        experts(0)
        with ExitStack() as attention:
            for name, shape, dt in (("xn_hi", [D, T], F32R), ("xn_lo", [D, T], F32R),
                                    ("kx", [D, B * KC], F32),
                                    ("xg_hi", [D, B, G], F32R), ("xg_lo", [D, B, G], F32R),
                                    ("gvo", [GH * G, B * H // GH, D], F32)):
                buf[name] = sb(name, shape, dt, attention)
            with ExitStack() as first:
                buf["xn_head"] = sb("xn_head", [CAND, B, D], F32, first)
                norm_stage(nc, buf, dram, "_n1", "pairs", "attend")
                select_stage(nc, buf, dram)
            global_values_stage(nc, buf, dram)
            attention_stage(nc, buf, dram)
        experts(2)
        norm_stage(nc, buf, dram, "_n3", "pairs", "store")


def kernel(**inputs):
    import concourse.bacc as bacc
    from concourse.bass_utils import run_bass_kernel_spmd

    a = {n.removeprefix("L0_"): np.asarray(v) for n, v in inputs.items()}
    by_head = lambda w: w.reshape(D, H, HD).transpose(2, 1, 0)
    w_up = a["ffn_wg"].transpose(0, 2, 1), a["ffn_wu"].transpose(0, 2, 1)
    w_down = a["ffn_wd"].transpose(0, 2, 1).reshape(E, J, P, D).transpose(0, 2, 1, 3).reshape(E, P, I)
    key, query = np.arange(WIN)[None, :], np.arange(WIN)[:, None]
    causal = np.where(key > query, np.float32(-3e38), np.float32(0)).astype(np.float32)
    arrays = {
        "x": a["attn_x"].reshape(T, D),
        "gate": a["ffn_gate_w"].T,
        "w_ffn": np.concatenate([*w_up, w_down], axis=2),
        "wq_t": by_head(a["attn_wq"]), "wk_t": by_head(a["attn_wk"]), "wv_t": by_head(a["attn_wv"]),
        "wo_t": a["attn_wo"].reshape(H, HD, D).transpose(1, 0, 2),
        "ws1": a["attn_ws1"], "bs1": a["attn_bs1"], "ws2": a["attn_ws2"], "bs2": a["attn_bs2"],
        "ident": np.eye(P, dtype=np.float32),
        "iota8": np.broadcast_to(np.arange(E, dtype=np.float32), (P, NT, E)),
        "lower": np.triu(np.ones((P, P), np.float32), 1),
        "ones": np.ones((P, P), np.float32),
        "iota_row": np.broadcast_to(np.arange(P, dtype=np.float32), (P, P)),
        "token": np.arange(T, dtype=np.float32).reshape(NT, P).T,
        "iota_tile": np.broadcast_to(np.arange(SLOT_TILES, dtype=np.float32)[None, :, None], (1, SLOT_TILES, E)),
        "iota_p": np.arange(CAND, dtype=np.float32)[:, None],
        "block_b": np.repeat(np.eye(B, dtype=np.float32)[:, :, None], G, axis=2),
        "mask": causal,
    }
    arrays = {n: np.ascontiguousarray(v) for n, v in arrays.items()}
    nc = bacc.Bacc("TRN2", target_bir_lowering=False, num_devices=1)
    dram = {n: nc.dram_tensor(f"in_{n}", v.shape, mybir.dt.from_np(v.dtype), kind="ExternalInput").ap()
            for n, v in arrays.items()}
    dram["out"] = nc.dram_tensor("out_x", [T, D], F32, kind="ExternalOutput").ap()
    macaron(nc, dram)
    r = run_bass_kernel_spmd(nc, [{f"in_{n}": v for n, v in arrays.items()}], core_ids=[0])
    return r.results[0]["out_x"].reshape(B, S, D)
```
